# Optimizing a Trainium2 kernel written in Bass

```python
import numpy as np
import jax
import jax.numpy as jnp

def _softmax(x, axis=-1):
    return jax.nn.softmax(x, axis=axis)

def _gelu(x):
    return jax.nn.gelu(x, approximate=True)

def _silu(x):
    return jax.nn.silu(x)

def _sigmoid(x):
    return jax.nn.sigmoid(x)

def _layernorm(x, axis=-1, eps=1e-05):
    m = jnp.mean(x, axis=axis, keepdims=True)
    v = jnp.var(x, axis=axis, keepdims=True)
    return (x - m) / jnp.sqrt(v + eps)

def _scatter_add(tgt, idx, src, axis=0):
    return tgt.at[idx].add(src)

def _segment_sum(src, seg, n):
    return jax.ops.segment_sum(src, seg, n)
kernel_name = 'mk_conv_seq_d2_conv_nchw256_r4_c5ac1e'

def setup_inputs(seed: int=0):
    np.random.seed(seed)
    _w = jnp.asarray

    def _rec_inputs():
        import jax
        import jax.numpy as jnp
        _gk = jax.random.key(seed)
        x = -0.0002928 + 1 * jax.random.normal(jax.random.fold_in(_gk, 1), (4, 64, 16, 16), jnp.float32)
        return x
    x = _rec_inputs()

    def _L0_conv_setup():
        import jax, jax.numpy as jnp
        import numpy as np
        GROUPS = 8
        EPS = 1e-05

        def group_norm(x, gamma, beta):
            B, C, H, W = x.shape
            xr = x.reshape(B, GROUPS, C // GROUPS, H * W)
            mu = xr.mean(axis=(2, 3), keepdims=True)
            var = xr.var(axis=(2, 3), keepdims=True)
            xn = (xr - mu) * jax.lax.rsqrt(var + EPS)
            xn = xn.reshape(B, C, H * W)
            return xn * gamma[None, :, None] + beta[None, :, None]
        key = jax.random.key(seed)
        k1, k2, k3 = jax.random.split(key, 3)
        B, C, H, W = (4, 64, 16, 16)
        x = jax.random.normal(k1, (B, C, H, W), dtype=jnp.float32)
        gamma = jnp.ones((C,), dtype=jnp.float32)
        beta = jnp.zeros((C,), dtype=jnp.float32)
        w_qkv = jax.random.normal(k2, (3 * C, C), dtype=jnp.float32) * C ** (-0.5)
        w_proj = jax.random.normal(k3, (C, C), dtype=jnp.float32) * C ** (-0.5)
        b_proj = jnp.zeros((C,), dtype=jnp.float32)
        return {'x': x, 'gamma': gamma, 'beta': beta, 'w_qkv': w_qkv, 'w_proj': w_proj, 'b_proj': b_proj}
    _L0_conv_all = _L0_conv_setup()
    _L0_conv_in = {k: v for k, v in _L0_conv_all.items() if k in ('gamma', 'beta', 'w_qkv', 'w_proj', 'b_proj')}
    del _L0_conv_all

    def _L1_conv_setup():
        import jax, jax.numpy as jnp
        import numpy as np
        D_MODEL = 64
        D_STATE = 32
        D_CONV = 4
        HEADDIM = 16
        NHEADS = D_MODEL // HEADDIM
        D_INNER = D_MODEL
        CONV_DIM = D_INNER + 2 * D_STATE
        D_IN_PROJ = 2 * D_INNER + 2 * D_STATE + NHEADS
        EPS = 1e-05

        def _mamba2_core(u, in_w, conv_w, conv_b, dt_bias, A_log, Dp, rms_w, out_w):
            b, L, _ = u.shape
            zxbcdt = jnp.einsum('bld,ed->ble', u, in_w)
            z = zxbcdt[..., :D_INNER]
            xBC = zxbcdt[..., D_INNER:D_INNER + CONV_DIM]
            dt = jax.nn.softplus(zxbcdt[..., -NHEADS:] + dt_bias)
            xc = jax.lax.conv_general_dilated(xBC.transpose(0, 2, 1), conv_w[:, None, :], (1,), [(D_CONV - 1, 0)], dimension_numbers=('NCH', 'OIH', 'NCH'), feature_group_count=CONV_DIM)
            xBC = jax.nn.silu((xc + conv_b[None, :, None]).transpose(0, 2, 1))
            xs = xBC[..., :D_INNER].reshape(b, L, NHEADS, HEADDIM)
            Bm = xBC[..., D_INNER:D_INNER + D_STATE]
            Cm = xBC[..., D_INNER + D_STATE:]
            A = -jnp.exp(A_log)

            def step(state, inp):
                dt_t, x_t, B_t, C_t = inp
                dA = jnp.exp(dt_t * A)
                state = state * dA[:, :, None, None] + (dt_t[:, :, None] * x_t)[..., None] * B_t[:, None, None, :]
                y_t = jnp.einsum('bhpn,bn->bhp', state, C_t)
                return (state, y_t)
            state0 = jnp.zeros((b, NHEADS, HEADDIM, D_STATE), u.dtype)
            _, ys = jax.lax.scan(step, state0, (dt.transpose(1, 0, 2), xs.transpose(1, 0, 2, 3), Bm.transpose(1, 0, 2), Cm.transpose(1, 0, 2)))
            y = ys.transpose(1, 0, 2, 3) + Dp[None, None, :, None] * xs
            y = y.reshape(b, L, D_INNER)
            y = y * jax.nn.silu(z)
            y = y * jax.lax.rsqrt(jnp.mean(y * y, axis=-1, keepdims=True) + EPS) * rms_w
            return jnp.einsum('bld,ed->ble', y, out_w)
        key = jax.random.key(seed)
        ks = jax.random.split(key, 12)
        b, h, w = (4, 32, 32)
        x = jax.random.normal(ks[0], (b, D_MODEL, h, w), jnp.float32)
        s = 0.02
        params = {'norm_g': jnp.ones((D_MODEL,), jnp.float32), 'norm_b': jnp.zeros((D_MODEL,), jnp.float32), 'in_w': jax.random.normal(ks[1], (D_IN_PROJ, D_MODEL), jnp.float32) * s, 'conv_w': jax.random.normal(ks[2], (CONV_DIM, D_CONV), jnp.float32) * 0.1, 'conv_b': jnp.zeros((CONV_DIM,), jnp.float32), 'dt_bias': jax.random.normal(ks[3], (NHEADS,), jnp.float32) * 0.1, 'A_log': jnp.log(jax.random.uniform(ks[4], (NHEADS,), jnp.float32, 1.0, 16.0)), 'Dp': jnp.ones((NHEADS,), jnp.float32), 'rms_w': jnp.ones((D_INNER,), jnp.float32), 'out_w': jax.random.normal(ks[5], (D_MODEL, D_INNER), jnp.float32) * s, 'se1_w': jax.random.normal(ks[6], (D_MODEL // 4, D_MODEL), jnp.float32) * s, 'se1_b': jnp.zeros((D_MODEL // 4,), jnp.float32), 'se2_w': jax.random.normal(ks[7], (D_MODEL, D_MODEL // 4), jnp.float32) * s, 'se2_b': jnp.zeros((D_MODEL,), jnp.float32)}
        return {'x': x, **params}
    _L1_conv_all = _L1_conv_setup()
    _L1_conv_in = {k: v for k, v in _L1_conv_all.items() if k in ('norm_g', 'norm_b', 'in_w', 'conv_w', 'conv_b', 'dt_bias', 'A_log', 'Dp', 'rms_w', 'out_w', 'se1_w', 'se1_b', 'se2_w', 'se2_b')}
    del _L1_conv_all
    return {'x': x, 'L0_conv_gamma': _L0_conv_in['gamma'], 'L0_conv_beta': _L0_conv_in['beta'], 'L0_conv_w_qkv': _L0_conv_in['w_qkv'], 'L0_conv_w_proj': _L0_conv_in['w_proj'], 'L0_conv_b_proj': _L0_conv_in['b_proj'], 'L1_conv_norm_g': _L1_conv_in['norm_g'], 'L1_conv_norm_b': _L1_conv_in['norm_b'], 'L1_conv_in_w': _L1_conv_in['in_w'], 'L1_conv_conv_w': _L1_conv_in['conv_w'], 'L1_conv_conv_b': _L1_conv_in['conv_b'], 'L1_conv_dt_bias': _L1_conv_in['dt_bias'], 'L1_conv_A_log': _L1_conv_in['A_log'], 'L1_conv_Dp': _L1_conv_in['Dp'], 'L1_conv_rms_w': _L1_conv_in['rms_w'], 'L1_conv_out_w': _L1_conv_in['out_w'], 'L1_conv_se1_w': _L1_conv_in['se1_w'], 'L1_conv_se1_b': _L1_conv_in['se1_b'], 'L1_conv_se2_w': _L1_conv_in['se2_w'], 'L1_conv_se2_b': _L1_conv_in['se2_b']}

def reference(x, L0_conv_gamma, L0_conv_beta, L0_conv_w_qkv, L0_conv_w_proj, L0_conv_b_proj, L1_conv_norm_g, L1_conv_norm_b, L1_conv_in_w, L1_conv_conv_w, L1_conv_conv_b, L1_conv_dt_bias, L1_conv_A_log, L1_conv_Dp, L1_conv_rms_w, L1_conv_out_w, L1_conv_se1_w, L1_conv_se1_b, L1_conv_se2_w, L1_conv_se2_b):
    import jax
    import jax.numpy as jnp

    def _L0_conv_ref(x, gamma, beta, w_qkv, w_proj, b_proj):
        import jax, jax.numpy as jnp
        import numpy as np
        GROUPS = 8
        EPS = 1e-05

        def group_norm(x, gamma, beta):
            B, C, H, W = x.shape
            xr = x.reshape(B, GROUPS, C // GROUPS, H * W)
            mu = xr.mean(axis=(2, 3), keepdims=True)
            var = xr.var(axis=(2, 3), keepdims=True)
            xn = (xr - mu) * jax.lax.rsqrt(var + EPS)
            xn = xn.reshape(B, C, H * W)
            return xn * gamma[None, :, None] + beta[None, :, None]
        B, C, H, W = x.shape
        N = H * W
        xn = group_norm(x, gamma, beta)
        qkv = jnp.einsum('oc,bcn->bon', w_qkv, xn)
        q, k, v = jnp.split(qkv, 3, axis=1)
        scores = jnp.einsum('bcn,bcm->bnm', q, k) * C ** (-0.5)
        attn = jax.nn.softmax(scores, axis=-1)
        out = jnp.einsum('bcm,bnm->bcn', v, attn)
        y = jnp.einsum('oc,bcn->bon', w_proj, out) + b_proj[None, :, None]
        return x + y.reshape(B, C, H, W)

    def _L1_conv_ref(x, norm_g, norm_b, in_w, conv_w, conv_b, dt_bias, A_log, Dp, rms_w, out_w, se1_w, se1_b, se2_w, se2_b):
        import jax, jax.numpy as jnp
        import numpy as np
        D_MODEL = 64
        D_STATE = 32
        D_CONV = 4
        HEADDIM = 16
        NHEADS = D_MODEL // HEADDIM
        D_INNER = D_MODEL
        CONV_DIM = D_INNER + 2 * D_STATE
        D_IN_PROJ = 2 * D_INNER + 2 * D_STATE + NHEADS
        EPS = 1e-05

        def _mamba2_core(u, in_w, conv_w, conv_b, dt_bias, A_log, Dp, rms_w, out_w):
            b, L, _ = u.shape
            zxbcdt = jnp.einsum('bld,ed->ble', u, in_w)
            z = zxbcdt[..., :D_INNER]
            xBC = zxbcdt[..., D_INNER:D_INNER + CONV_DIM]
            dt = jax.nn.softplus(zxbcdt[..., -NHEADS:] + dt_bias)
            xc = jax.lax.conv_general_dilated(xBC.transpose(0, 2, 1), conv_w[:, None, :], (1,), [(D_CONV - 1, 0)], dimension_numbers=('NCH', 'OIH', 'NCH'), feature_group_count=CONV_DIM)
            xBC = jax.nn.silu((xc + conv_b[None, :, None]).transpose(0, 2, 1))
            xs = xBC[..., :D_INNER].reshape(b, L, NHEADS, HEADDIM)
            Bm = xBC[..., D_INNER:D_INNER + D_STATE]
            Cm = xBC[..., D_INNER + D_STATE:]
            A = -jnp.exp(A_log)

            def step(state, inp):
                dt_t, x_t, B_t, C_t = inp
                dA = jnp.exp(dt_t * A)
                state = state * dA[:, :, None, None] + (dt_t[:, :, None] * x_t)[..., None] * B_t[:, None, None, :]
                y_t = jnp.einsum('bhpn,bn->bhp', state, C_t)
                return (state, y_t)
            state0 = jnp.zeros((b, NHEADS, HEADDIM, D_STATE), u.dtype)
            _, ys = jax.lax.scan(step, state0, (dt.transpose(1, 0, 2), xs.transpose(1, 0, 2, 3), Bm.transpose(1, 0, 2), Cm.transpose(1, 0, 2)))
            y = ys.transpose(1, 0, 2, 3) + Dp[None, None, :, None] * xs
            y = y.reshape(b, L, D_INNER)
            y = y * jax.nn.silu(z)
            y = y * jax.lax.rsqrt(jnp.mean(y * y, axis=-1, keepdims=True) + EPS) * rms_w
            return jnp.einsum('bld,ed->ble', y, out_w)
        b, c, h, w = x.shape
        L = h * w
        u = x.transpose(0, 2, 3, 1).reshape(b, L, c)
        mu = jnp.mean(u, axis=-1, keepdims=True)
        var = jnp.mean((u - mu) ** 2, axis=-1, keepdims=True)
        u = (u - mu) * jax.lax.rsqrt(var + EPS) * norm_g + norm_b
        out = _mamba2_core(u, in_w, conv_w, conv_b, dt_bias, A_log, Dp, rms_w, out_w)
        out_img = out.reshape(b, h, w, c).transpose(0, 3, 1, 2)
        pooled = jnp.mean(out_img, axis=(2, 3))
        hdn = jax.nn.relu(pooled @ se1_w.T + se1_b)
        attn = jax.nn.sigmoid(hdn @ se2_w.T + se2_b)
        return x + out_img * attn[:, :, None, None]

    def _gn(v, G=32, eps=1e-05):
        B_, C_, H_, W_ = v.shape
        g = v.reshape(B_, G, C_ // G, H_, W_)
        m = jnp.mean(g, axis=(2, 3, 4), keepdims=True)
        s = jnp.var(g, axis=(2, 3, 4), keepdims=True)
        return ((g - m) / jnp.sqrt(s + eps)).reshape(v.shape)

    def _ln_c(v, eps=1e-06):
        m = jnp.mean(v, axis=1, keepdims=True)
        s = jnp.var(v, axis=1, keepdims=True)
        return (v - m) / jnp.sqrt(s + eps)

    def _ln_t(v, eps=1e-05):
        m = jnp.mean(v, axis=-1, keepdims=True)
        s = jnp.var(v, axis=-1, keepdims=True)
        return (v - m) / jnp.sqrt(s + eps)

    def _to_tokens(v):
        B_, C_, H_, W_ = v.shape
        return v.reshape(B_, C_, H_ * W_).transpose(0, 2, 1)

    def _from_tokens(t, like):
        B_, C_, H_, W_ = like.shape
        return t.transpose(0, 2, 1).reshape(B_, C_, H_, W_)
    x = _L0_conv_ref(x, L0_conv_gamma, L0_conv_beta, L0_conv_w_qkv, L0_conv_w_proj, L0_conv_b_proj)
    x = _L1_conv_ref(x, L1_conv_norm_g, L1_conv_norm_b, L1_conv_in_w, L1_conv_conv_w, L1_conv_conv_b, L1_conv_dt_bias, L1_conv_A_log, L1_conv_Dp, L1_conv_rms_w, L1_conv_out_w, L1_conv_se1_w, L1_conv_se1_b, L1_conv_se2_w, L1_conv_se2_b)
    return x

_drawn_inputs = setup_inputs


def setup_inputs(seed=0):
    import zlib

    import numpy as np

    out = dict(_drawn_inputs(seed))
    spreads = {'L0_conv_gamma': (1.0, 0.2),
     'L0_conv_beta': (0.0, 0.1),
     'L0_conv_b_proj': (0.0, 0.1),
     'L1_conv_norm_g': (1.0, 0.6),
     'L1_conv_norm_b': (0.0, 0.8),
     'L1_conv_conv_b': (0.0, 0.1),
     'L1_conv_Dp': (1.0, 0.6),
     'L1_conv_rms_w': (1.0, 0.6),
     'L1_conv_se1_b': (0.0, 2.0),
     'L1_conv_se2_b': (0.0, 0.8)}
    factors = {'L1_conv_dt_bias': 64.0,
     'L1_conv_A_log': 8.0,
     'L1_conv_se1_w': 64.0,
     'L1_conv_se2_w': 24.942}
    for name, (base, spread) in spreads.items():
        noise = np.random.default_rng([zlib.crc32(name.encode()), seed]).standard_normal(out[name].shape)
        drawn = base * np.exp(spread * noise) if base else spread * noise
        out[name] = jnp.asarray(drawn.astype(out[name].dtype))
    for name, factor in factors.items():
        out[name] = (out[name] * factor).astype(out[name].dtype)
    return out
```

```python
import concourse.bass as bass
from concourse import mybir
from contextlib import ExitStack
import math

B, C, N = 4, 64, 256
BP = 2
PAIRS = B // BP
T = 128
NT = N // T
K = NT * BP
GROUP = C // 8
NH, HD, DS = 4, 16, 32
TAPS = 4
HID = C // 4
ZD = C + NH
UP = N + TAPS
EPS = 1e-5

E_GAMMA, E_BETA, E_WQ, E_WK, E_WV, E_WPT, E_BPROJ = 0, 1, 2, 66, 194, 322, 386
E_COLS = 450
L_NG, L_NB, L_RMS, L_D, L_CONVB, L_SE2B, L_SE1B = 0, 1, 2, 3, 4, 5, 6
L_CONVW, L_DTB, L_ALOG, L_INW, L_WZDT = 8, 12, 16, 20, 84
L_OUTW, L_OUTWT, L_SE1T, L_SE2T = 152, 280, 408, 424
L_COLS = 552


def artanh_coefficients(degree):
    import numpy as np
    k = np.arange(64)
    w = (1 + np.cos(np.pi * (k + 0.5) / 64)) / 18
    z = np.sqrt(w)
    fit = np.polynomial.chebyshev.Chebyshev.fit(w, 2 * np.arctanh(z) / z, degree, domain=[0, 1 / 9])
    return [float(c) for c in fit.convert(kind=np.polynomial.Polynomial).coef]


def attention_mamba_kernel(nc: bass.Bass, x: bass.AP, early: bass.AP, late: bass.AP, out: bass.AP):
    fp32 = mybir.dt.float32
    ALU = mybir.AluOpType
    ACT = mybir.ActivationFunctionType
    AX = mybir.AxisListType
    ART = artanh_coefficients(4)

    x_v = x.rearrange("(p b) c h w -> p (b c) (h w)", b=BP)
    out_v = out.rearrange("(p b) c h w -> p (b c) (h w)", b=BP)

    ctx = ExitStack()
    with ctx:
        def sb(name, shape):
            return ctx.enter_context(nc.sbuf_tensor(name, shape, fp32))

        def sem(name):
            return ctx.enter_context(nc.semaphore(name))

        xc = sb("xc", [128, PAIRS, N])
        pe_ = sb("params_early", [128, E_COLS])
        pl = sb("params_late", [128, L_COLS])
        ident = sb("ident", [128, 128])
        group_mean = sb("group_mean", [128, 128])
        after = sb("after", [128, 128])
        upto = sb("upto", [128, 128])
        minus_half = sb("minus_half", [128, 4])

        mix = sb("mix", [128, 2, 128])
        conv_in = sb("conv_in", [128, TAPS, C])
        conv_w = sb("conv_w", [128, 2, 128])
        diag_d = sb("diag_d", [C, C])
        se1 = sb("se1", [128, BP * HID])
        neg_a = sb("neg_a", [128, NH])
        half_bias = sb("half_bias", [128, 2])

        gst = sb("gst", [128, PAIRS, 6])
        gmv = sb("gmv", [128, PAIRS, 2])
        gmq = sb("gmq", [128, 2, PAIRS])
        gsq = sb("gsq", [128, PAIRS])
        gg = sb("gg", [128, 2, PAIRS])
        gve = sb("gve", [128, PAIRS])
        grs = sb("grs", [128, PAIRS])
        gscale = sb("gscale", [128, PAIRS])
        gms = sb("gms", [128, PAIRS])
        gshift = sb("gshift", [128, PAIRS])
        xn = sb("xn", [128, PAIRS, N])

        keys = sb("keys", [128, PAIRS, N])
        vals = sb("vals", [128, PAIRS, K, C + 1])
        xT = sb("xT", [128, PAIRS, K, C])
        neg_max = sb("neg_max", [128, PAIRS, BP, NT])
        prob = sb("prob", [128, PAIRS, BP, NT, N])
        probT = sb("probT", [128, PAIRS, BP, NT, N])
        rden = sb("rden", [128, PAIRS, K])
        ynorm = sb("ynorm", [128, PAIRS, K, C])
        h = sb("h", [128, PAIRS, K, C])
        hT = sb("hT", [128, PAIRS, N])

        lst = sb("lst", [128, PAIRS, K, 6])
        lmv = sb("lmv", [128, PAIRS, K, 2])
        lve = sb("lve", [128, PAIRS, K])
        lrs = sb("lrs", [128, PAIRS, K])
        u = sb("u", [128, PAIRS, K, 2, C])
        uc = sb("uc", [128, PAIRS, BP, UP])
        half_v = sb("half_v", [128, PAIRS, BP, N])
        half_t = sb("half_t", [128, PAIRS, BP, N])
        s = sb("s", [128, PAIRS, BP, N])
        cs = sb("cs", [128, PAIRS, BP, N])
        zt = sb("zt", [128, PAIRS, K, C])
        zg = sb("zg", [128, PAIRS, K, C])

        dx = sb("dx", [128, PAIRS, K, NH])
        dn = sb("dn", [128, PAIRS, K * NH])
        de = sb("de", [128, PAIRS, K * NH])
        dd = sb("dd", [128, PAIRS, K * NH])
        dr = sb("dr", [128, PAIRS, K * NH])
        dz = sb("dz", [128, PAIRS, K * NH])
        dw = sb("dw", [128, PAIRS, K * NH])
        dq = sb("dq", [128, PAIRS, 2, K * NH])
        dt = sb("dt", [128, PAIRS, K, NH])
        a = sb("a", [128, PAIRS, K, NH])

        am = sb("am", [128, PAIRS, K, NH, T])
        decay = sb("decay", [128, PAIRS, K, NH, T])
        gm = sb("gm", [128, PAIRS, K, T])
        att = sb("att", [128, PAIRS, K, NH, T])
        dtx = sb("dtx", [128, PAIRS, K, C])
        bT = sb("bT", [128, PAIRS, BP, DS])
        wdtx = sb("wdtx", [128, PAIRS, BP, C])
        state = sb("state", [128, PAIRS, BP, C])
        carry = sb("carry", [128, PAIRS, BP, NH])
        yc = sb("yc", [128, PAIRS, BP, C])
        ys = sb("ys", [128, PAIRS, BP, C])

        y2 = sb("y2", [128, PAIRS, K, C])
        ysq = sb("ysq", [128, PAIRS, K, C])
        yss = sb("yss", [128, PAIRS, K])
        yve = sb("yve", [128, PAIRS, K])
        yrs = sb("yrs", [128, PAIRS, K])
        y3 = sb("y3", [128, PAIRS, K, C])
        y3T = sb("y3T", [128, PAIRS, N])
        ysum = sb("ysum", [128, PAIRS])
        hidden = sb("hidden", [BP * HID, PAIRS])
        gate_t = sb("gate_t", [128, PAIRS])
        gate = sb("gate", [128, PAIRS])
        res = sb("res", [128, PAIRS, N])

        bank = [ctx.enter_context(nc.psum_tensor(f"bank{i}", [128, 512], fp32)) for i in range(8)]
        ps_setup = bank[7]
        ps_xT = bank[6]
        ps_proj = bank[0]
        ps_score = [bank[1], bank[2]]
        ps_probT = [bank[3], bank[4]]
        ps_y = bank[5]
        ps_uT = bank[6]
        ps_conv = bank[7]
        ps_zdt = bank[0]
        ps_sT = bank[6]
        ps_G = bank[7]
        ps_S = [bank[1], bank[2], bank[3], bank[4]]
        ps_ys = bank[5]
        ps_mid = bank[6]
        ps_y3T = bank[7]
        ps_out = bank[7]
        ps_se = bank[0]

        s_x = [sem(f"s_x{p}") for p in range(PAIRS)]
        s_early, s_late, s_out = sem("s_early"), sem("s_late"), sem("s_out")
        s_zero, s_ident, s_group, s_masks = sem("s_zero"), sem("s_ident"), sem("s_group"), sem("s_masks")
        s_mixp, s_mix = sem("s_mixp"), sem("s_mix")
        s_gmq, s_gg, s_gve, s_grs = sem("s_gmq"), sem("s_gg"), sem("s_gve"), sem("s_grs")
        s_ggread = sem("s_ggread")
        s_gshift, s_xn = sem("s_gshift"), sem("s_xn")
        s_xTp, s_xT = sem("s_xTp"), sem("s_xT")
        s_keysp, s_valsp, s_keys, s_vals = sem("s_keysp"), sem("s_valsp"), sem("s_keys"), sem("s_vals")
        s_score, s_max, s_prob, s_probTp = sem("s_score"), sem("s_max"), sem("s_prob"), sem("s_probTp")
        s_probT0, s_probT1 = sem("s_probT0"), sem("s_probT1")
        s_y, s_yread, s_h, s_hTp, s_hT = sem("s_y"), sem("s_yread"), sem("s_h"), sem("s_hTp"), sem("s_hT")
        s_lve, s_lrs, s_u, s_uTp = sem("s_lve"), sem("s_lrs"), sem("s_u"), sem("s_uTp")
        s_uclo, s_uchi = sem("s_uclo"), sem("s_uchi")
        s_convin, s_wconvp, s_wconv, s_se1p, s_se1 = (sem("s_convin"), sem("s_wconvp"), sem("s_wconv"),
                                                      sem("s_se1p"), sem("s_se1"))
        s_aexp, s_nega, s_diag, s_half = sem("s_aexp"), sem("s_nega"), sem("s_diag"), sem("s_half")
        s_conv, s_half_v, s_half_t, s_s, s_cs = (sem("s_conv"), sem("s_half_v"), sem("s_half_t"),
                                                 sem("s_s"), sem("s_cs"))
        s_zdt, s_zt, s_zg, s_dx = sem("s_zdt"), sem("s_zt"), sem("s_zg"), sem("s_dx")
        s_dn, s_de, s_dt, s_a = sem("s_dn"), sem("s_de"), sem("s_dt"), sem("s_a")
        s_am, s_S, s_decay = sem("s_am"), sem("s_S"), sem("s_decay")
        s_sT, s_dtx, s_bT, s_G, s_gm, s_att = (sem("s_sT"), sem("s_dtx"), sem("s_bT"), sem("s_G"),
                                               sem("s_gm"), sem("s_att"))
        s_wdtx, s_statep, s_state, s_carryp, s_carry = (sem("s_wdtx"), sem("s_statep"), sem("s_state"),
                                                        sem("s_carryp"), sem("s_carry"))
        s_inter, s_ys, s_yc, s_y2 = sem("s_inter"), sem("s_ys"), sem("s_yc"), sem("s_y2")
        s_yve, s_yrs, s_y3, s_y3Tp, s_y3T = sem("s_yve"), sem("s_yrs"), sem("s_y3"), sem("s_y3Tp"), sem("s_y3T")
        s_outp, s_hidp, s_hid, s_gatep, s_gatet = (sem("s_outp"), sem("s_hidp"), sem("s_hid"),
                                                   sem("s_gatep"), sem("s_gatet"))
        s_res = sem("s_res")
        s_vec, s_act = sem("s_vec"), sem("s_act")
        s_bn = sem("s_bn")

        block = ctx.enter_context(nc.Block())

        @block.sync
        def _(sync):
            sync.dma_start(xc[:, 0, :], x_v[0]).then_inc(s_x[0], 16)
            sync.dma_start(pe_[:, :], early).then_inc(s_early, 16)
            for p in range(PAIRS):
                sync.wait_ge(s_res, p + 1)
                sync.dma_start(out_v[p], res[:, p, :]).then_inc(s_out, 16)
            sync.wait_ge(s_out, 16 * PAIRS)

        @block.gpsimd
        def _(pool):
            def mark(ap, value, keep, compare, base, pattern, channel):
                return nc.gpsimd.affine_select(out=ap, in_=ap, compare_op=compare, fill=value, base=base,
                                               pattern=pattern, channel_multiplier=channel)

            nc.gpsimd.memset(group_mean[:, :], 1.0 / GROUP).then_inc(s_zero, 1)
            nc.gpsimd.memset(ident[:, :], 0.0).then_inc(s_zero, 1)
            nc.gpsimd.memset(minus_half[:, :], -0.5).then_inc(s_zero, 1)
            nc.gpsimd.memset(mix[:, :, :], 0.0).then_inc(s_zero, 1)
            pool.wait_ge(s_zero, 4)
            gv = group_mean[:, :].rearrange("c (g j) -> c g j", j=GROUP)
            gpat = [[-GROUP, 128 // GROUP], [0, GROUP]]
            mark(gv, 0.0, True, ALU.is_ge, 0, gpat, 1).then_inc(s_group, 1)
            pool.wait_ge(s_group, 1)
            nc.gpsimd.affine_select(out=gv, in_=gv, compare_op=ALU.is_ge, fill=0.0, base=GROUP - 1,
                                    pattern=[[GROUP, 128 // GROUP], [0, GROUP]],
                                    channel_multiplier=-1).then_inc(s_group, 1)
            nc.gpsimd.affine_select(out=ident[:, :], in_=ident[:, :], compare_op=ALU.not_equal, fill=1.0,
                                    base=0, pattern=[[-1, 128]], channel_multiplier=1).then_inc(s_ident, 1)
            pool.wait_ge(s_gve, 1)
            nc.gpsimd.tensor_tensor(grs[:, :], gve[:, :], minus_half[:, 0:PAIRS], ALU.pow).then_inc(s_grs, 1)
            nc.gpsimd.memset(after[:, :], 1.0).then_inc(s_zero, 1)
            nc.gpsimd.memset(upto[:, :], 1.0).then_inc(s_zero, 1)
            nc.gpsimd.memset(se1[:, :], 0.0).then_inc(s_zero, 1)
            nc.gpsimd.memset(uc[:, :, :, 0:TAPS - 1], 0.0).then_inc(s_zero, 1)
            nc.gpsimd.memset(vals[:, :, :, C:C + 1], 1.0).then_inc(s_zero, 1)
            pool.wait_ge(s_zero, 9)
            nc.gpsimd.affine_select(out=after[:, :], in_=after[:, :], compare_op=ALU.is_gt, fill=0.0, base=0,
                                    pattern=[[-1, 128]], channel_multiplier=1).then_inc(s_masks, 1)
            nc.gpsimd.affine_select(out=upto[:, :], in_=upto[:, :], compare_op=ALU.is_ge, fill=0.0, base=0,
                                    pattern=[[1, 128]], channel_multiplier=-1).then_inc(s_masks, 1)

            def layer_rstd(p):
                pool.wait_ge(s_lve, p + 1)
                nc.gpsimd.tensor_tensor(lrs[:, p, :], lve[:, p, :], minus_half[:, 0:K], ALU.pow)\
                    .then_inc(s_lrs, 1)

            def masked_decay(p):
                pool.wait_ge(s_a, p + 1)
                for k in range(K):
                    nc.gpsimd.affine_select(
                        out=am[:, p, k, :, :], in_=a[:, p, k, :].unsqueeze(2).to_broadcast([128, NH, T]),
                        compare_op=ALU.is_ge, fill=0.0, base=0, pattern=[[0, NH], [1, T]],
                        channel_multiplier=-1).then_inc(s_am, 1)

            def rms_rstd(p):
                pool.wait_ge(s_yve, p + 1)
                nc.gpsimd.tensor_tensor(yrs[:, p, :], yve[:, p, :], minus_half[:, 0:K], ALU.pow)\
                    .then_inc(s_yrs, 1)

            layer_rstd(0)
            layer_rstd(1)
            masked_decay(0)
            masked_decay(1)
            rms_rstd(0)
            rms_rstd(1)

        @block.scalar
        def _(act):
            done = [0]

            def link(ins):
                done[0] += 1
                ins.then_inc(s_act, 1)
                act.wait_ge(s_act, done[0])

            act.dma_start(xc[:, 1, :], x_v[1]).then_inc(s_x[1], 16)
            act.dma_start(pl[:, :], late).then_inc(s_late, 16)

            act.wait_ge(s_mixp, 1)
            act.wait_ge(s_zero, 4)
            mp = ps_setup[:, 0:2 * C].rearrange("p (m c) -> p m c", m=2)
            for b in range(BP):
                nc.scalar.activation(mix[C * b:C * b + C, :, C * b:C * b + C], mp[C * b:C * b + C, :, :],
                                     ACT.Copy).then_inc(s_mix, 1)
            act.wait_ge(s_late, 16)
            link(nc.scalar.activation(neg_a[:, :], pl[:, L_ALOG:L_ALOG + NH], ACT.Exp))
            nc.scalar.mul(neg_a[:, :], neg_a[:, :], -1.0).then_inc(s_nega, 1)
            nc.scalar.mul(half_bias[:, :], pl[:, L_CONVB:L_CONVB + 2], 0.5).then_inc(s_half, 1)

            def keys_values(p):
                act.wait_ge(s_keysp, p + 1)
                nc.scalar.activation(keys[:, p, :], ps_proj[:, 0:N], ACT.Copy, scale=C ** -0.5)\
                    .then_inc(s_keys, 1)
                act.wait_ge(s_valsp, p + 1)
                nc.scalar.activation(vals[:, p, :, 0:C],
                                     ps_proj[:, N:2 * N].rearrange("p (k c) -> p k c", k=K), ACT.Copy)\
                    .then_inc(s_vals, 1)

            def softmax(p, b):
                act.wait_ge(s_max, BP * p + b + 1)
                for i in range(NT):
                    nc.scalar.activation(prob[:, p, b, i, :], ps_score[b][:, N * i:N * i + N], ACT.Exp,
                                         bias=neg_max[:, p, b, i:i + 1]).then_inc(s_prob, 1)

            def probT_copy(p):
                act.wait_ge(s_probTp, BP * p + 2)
                nc.scalar.activation(probT[:, p, 1, :, :].rearrange("p i n -> p (i n)"), ps_probT[1][:, :],
                                     ACT.Copy).then_inc(s_probT1, 1)

            def h_copy(p):
                act.wait_ge(s_hTp, p + 1)
                nc.scalar.activation(hT[:, p, :], ps_y[:, 0:N], ACT.Copy).then_inc(s_hT, 1)

            def layer_affine(p):
                if p == 0:
                    act.wait_ge(s_zero, 8)
                act.wait_ge(s_uTp, p + 1)
                nc.scalar.activation(uc[0:C, p, :, TAPS - 1:TAPS - 1 + N],
                                     ps_uT[0:C, :].rearrange("p (b n) -> p b n", b=BP), ACT.Identity,
                                     scale=pl[0:C, L_NG:L_NG + 1], bias=pl[0:C, L_NB:L_NB + 1])\
                    .then_inc(s_uclo, 1)

            def gate_tanh(p):
                act.wait_ge(s_zdt, p + 1)
                act.wait_ge(s_dx, p + 1)
                nc.scalar.activation(zt[:, p, :, :],
                                     ps_zdt[:, 0:K * ZD].rearrange("p (k z) -> p k z", k=K)[:, :, 0:C],
                                     ACT.Tanh, scale=0.5).then_inc(s_zt, 1)

            def conv_silu(p):
                if p == 0:
                    act.wait_ge(s_half, 1)
                act.wait_ge(s_conv, p + 1)
                cv = ps_conv[:, :]
                nc.scalar.activation(half_t[:, p, :, :].rearrange("p b n -> p (b n)"), cv, ACT.Tanh,
                                     scale=0.5, bias=half_bias[:, 0:1]).then_inc(s_half_t, 1)
                nc.scalar.activation(half_v[:, p, :, :].rearrange("p b n -> p (b n)"), cv, ACT.Identity,
                                     scale=0.5, bias=half_bias[:, 0:1]).then_inc(s_half_v, 1)

            def dt_exp(p):
                act.wait_ge(s_dn, p + 1)
                nc.scalar.activation(de[:, p, :], dn[:, p, :], ACT.Exp).then_inc(s_de, 1)

            def decays(p, k):
                act.wait_ge(s_S, K * p + k + 1)
                nc.scalar.activation(decay[:, p, k, :, :].rearrange("p h t -> p (h t)"), ps_S[k][:, :],
                                     ACT.Exp).then_inc(s_decay, 1)

            def chunk_state(p):
                act.wait_ge(s_statep, p + 1)
                nc.scalar.activation(state[C:C + DS, p, :, :].rearrange("p b c -> p (b c)"),
                                     ps_mid[C:C + DS, 0:BP * C], ACT.Copy).then_inc(s_state, 1)
                nc.scalar.activation(carry[:, p, :, :].rearrange("p b h -> p (b h)"),
                                     ps_mid[:, 256:256 + BP * NH], ACT.Exp).then_inc(s_carry, 1)

            def rms_weight(p):
                act.wait_ge(s_y3Tp, p + 1)
                nc.scalar.activation(y3T[:, p, :], ps_y3T[:, 0:N], ACT.Copy,
                                     scale=pl[:, L_RMS:L_RMS + 1], accum_out=ysum[:, p:p + 1])\
                    .then_inc(s_y3T, 1)

            def squeeze(p):
                act.wait_ge(s_hidp, p + 1)
                nc.scalar.activation(hidden[:, p:p + 1], ps_se[0:BP * HID, 0:1], ACT.Relu, scale=1.0 / N,
                                     bias=pl[0:BP * HID, L_SE1B:L_SE1B + 1]).then_inc(s_hid, 1)
                act.wait_ge(s_gatep, p + 1)
                nc.scalar.activation(gate_t[:, p:p + 1], ps_se[:, 1:2], ACT.Tanh, scale=0.5,
                                     bias=half_bias[:, 1:2]).then_inc(s_gatet, 1)

            keys_values(0)
            keys_values(1)
            softmax(0, 0)
            softmax(0, 1)
            probT_copy(0)
            softmax(1, 0)
            softmax(1, 1)
            h_copy(0)
            layer_affine(0)
            probT_copy(1)
            dt_exp(0)
            conv_silu(0)
            gate_tanh(0)
            h_copy(1)
            layer_affine(1)
            for k in range(K):
                decays(0, k)
            dt_exp(1)
            conv_silu(1)
            gate_tanh(1)
            chunk_state(0)
            for k in range(K):
                decays(1, k)
            rms_weight(0)
            squeeze(0)
            chunk_state(1)
            rms_weight(1)
            squeeze(1)

        @block.vector
        def _(dve):
            done = [0]

            def link(ins):
                done[0] += 1
                ins.then_inc(s_vec, 1)
                dve.wait_ge(s_vec, done[0])

            for p in range(PAIRS):
                dve.wait_ge(s_x[p], 16)
                nc.vector.bn_stats(gst[:, p, :], xc[:, p, :]).then_inc(s_vec, 1)
                done[0] += 1
            for p in range(PAIRS):
                dve.wait_ge(s_vec, p + 1)
                last = nc.vector.bn_aggr(gmv[:, p, :], gst[:, p, :])
                last.then_inc(s_vec, 1)
                done[0] += 1
            dve.wait_ge(s_vec, done[0])
            mean_c, var_c = gmv[:, :, 0], gmv[:, :, 1]
            nc.vector.tensor_copy(gmq[:, 0, :], mean_c)
            link(nc.vector.tensor_tensor(gsq[:, :], mean_c, mean_c, ALU.mult))
            nc.vector.tensor_tensor(gmq[:, 1, :], gsq[:, :], var_c, ALU.add).then_inc(s_gmq, 1)
            dve.wait_ge(s_gg, 1)
            link(nc.vector.tensor_copy(gg[:, :, :].rearrange("p m b -> p (m b)"),
                                       ps_setup[:, 128:128 + 2 * PAIRS]))
            link(nc.vector.tensor_tensor(gsq[:, :], gg[:, 0, :], gg[:, 0, :], ALU.mult))
            nc.vector.scalar_tensor_tensor(gve[:, :], gg[:, 1, :], EPS, gsq[:, :], ALU.add, ALU.subtract)\
                .then_inc(s_gve, 1)
            dve.wait_ge(s_early, 16)
            dve.wait_ge(s_grs, 1)
            link(nc.vector.tensor_scalar(gscale[:, :], grs[:, :], pe_[:, E_GAMMA:E_GAMMA + 1], None, ALU.mult))
            link(nc.vector.tensor_tensor(gms[:, :], gg[:, 0, :], gscale[:, :], ALU.mult))
            link(nc.vector.tensor_scalar(gshift[:, :], gms[:, :], -1.0, pe_[:, E_BETA:E_BETA + 1],
                                         ALU.mult, ALU.add))
            for p in range(PAIRS):
                nc.vector.tensor_scalar(xn[:, p, :], xc[:, p, :], gscale[:, p:p + 1], gshift[:, p:p + 1],
                                        ALU.mult, ALU.add).then_inc(s_xn, 1)

            for p in range(PAIRS):
                dve.wait_ge(s_xTp, PAIRS)
                nc.vector.tensor_tensor(
                    xT[:, p, :, :], ps_xT[:, N * p:N * p + N].rearrange("p (k c) -> p k c", k=K),
                    pe_[:, E_BPROJ:E_BPROJ + C].unsqueeze(1).to_broadcast([128, K, C]), ALU.add)\
                    .then_inc(s_xT, 1)

            def row_max(p, b):
                dve.wait_ge(s_score, NT * (BP * p + b) + NT)
                nc.vector.tensor_reduce(neg_max[:, p, b, :], ps_score[b][:, :].rearrange("p (i m) -> p i m", i=NT),
                                        AX.X, ALU.max, negate=True).then_inc(s_max, 1)

            def probT_copy(p):
                dve.wait_ge(s_probTp, BP * p + 1)
                nc.vector.tensor_copy(probT[:, p, 0, :, :].rearrange("p i n -> p (i n)"), ps_probT[0][:, :])\
                    .then_inc(s_probT0, 1)

            def residual(p):
                dve.wait_ge(s_y, p + 1)
                yv = ps_y[:, 0:K * (C + 1)].rearrange("p (k c) -> p k c", k=K)
                link(nc.vector.reciprocal(rden[:, p, :], yv[:, :, C]))
                nc.vector.tensor_tensor(ynorm[:, p, :, :], yv[:, :, 0:C],
                                        rden[:, p, :].unsqueeze(2).to_broadcast([128, K, C]), ALU.mult)\
                    .then_inc(s_yread, 1)
                dve.wait_ge(s_yread, p + 1)
                dve.wait_ge(s_xT, PAIRS)
                nc.vector.tensor_tensor(h[:, p, :, :], ynorm[:, p, :, :], xT[:, p, :, :], ALU.add)\
                    .then_inc(s_h, 1)

            def layer_norm(p):
                dve.wait_ge(s_h, p + 1)
                for k in range(K):
                    nc.vector.bn_stats(lst[:, p, k, :], h[:, p, k, :]).then_inc(s_bn, 1)
                for k in range(K):
                    dve.wait_ge(s_bn, 2 * K * p + k + 1)
                    nc.vector.bn_aggr(lmv[:, p, k, :], lst[:, p, k, :]).then_inc(s_bn, 1)
                dve.wait_ge(s_bn, 2 * K * (p + 1))
                nc.vector.tensor_scalar(lve[:, p, :], lmv[:, p, :, 1], EPS, None, ALU.add).then_inc(s_lve, 1)

            def layer_scale(p):
                dve.wait_ge(s_lrs, p + 1)
                for k in range(K):
                    nc.vector.tensor_scalar(u[:, p, k, :, :],
                                            h[:, p, k, :].unsqueeze(1).to_broadcast([128, 2, C]), lmv[:, p, k, 0:1],
                                            lrs[:, p, k:k + 1], ALU.subtract, ALU.mult).then_inc(s_u, 1)

            def layer_affine(p):
                if p == 0:
                    dve.wait_ge(s_zero, 8)
                dve.wait_ge(s_uTp, p + 1)
                nc.vector.tensor_scalar(uc[C:2 * C, p, :, TAPS - 2:TAPS - 2 + N],
                                        ps_uT[C:2 * C, :].rearrange("p (b n) -> p b n", b=BP),
                                        pl[C:2 * C, L_NG:L_NG + 1], pl[C:2 * C, L_NB:L_NB + 1],
                                        ALU.mult, ALU.add).then_inc(s_uchi, 1)

            def weights():
                dve.wait_ge(s_late, 16)
                dve.wait_ge(s_ident, 1)
                nc.vector.tensor_tensor(
                    conv_in[:, :, :], pl[:, L_INW:L_INW + C].unsqueeze(1).to_broadcast([128, TAPS, C]),
                    pl[:, L_CONVW:L_CONVW + TAPS].unsqueeze(2).to_broadcast([128, TAPS, C]), ALU.mult)\
                    .then_inc(s_convin, 1)
                nc.vector.tensor_scalar(diag_d[:, :], ident[0:C, 0:C], pl[0:C, L_D:L_D + 1], None, ALU.mult)\
                    .then_inc(s_diag, 1)
                dve.wait_ge(s_wconvp, 1)
                nc.vector.tensor_copy(conv_w[:, :, :].rearrange("p k c -> p (k c)"), ps_setup[:, 0:256])\
                    .then_inc(s_wconv, 1)
                dve.wait_ge(s_zero, 9)
                for b in range(BP):
                    nc.vector.tensor_copy(se1[C * b:C * b + C, HID * b:HID * b + HID],
                                          ps_setup[C * b:C * b + C, 256:256 + HID]).then_inc(s_se1, 1)

            def dt_argument(p):
                dve.wait_ge(s_zdt, p + 1)
                zv = ps_zdt[:, 0:K * ZD].rearrange("p (k z) -> p k z", k=K)
                nc.vector.tensor_tensor(dx[:, p, :, :], zv[:, :, C:ZD],
                                        pl[:, L_DTB:L_DTB + NH].unsqueeze(1).to_broadcast([128, K, NH]),
                                        ALU.add).then_inc(s_dx, 1)
                dve.wait_ge(s_dx, p + 1)
                dxf = dx[:, p, :, :].rearrange("p k h -> p (k h)")
                nc.vector.scalar_tensor_tensor(dn[:, p, :], dxf, -1.0, dxf, ALU.mult, ALU.min)\
                    .then_inc(s_dn, 1)

            def softplus(p):
                dve.wait_ge(s_de, p + 1)
                e, d, r, z, w = de[:, p, :], dd[:, p, :], dr[:, p, :], dz[:, p, :], dw[:, p, :]
                q = [dq[:, p, 0, :], dq[:, p, 1, :]]
                link(nc.vector.tensor_scalar(d, e, 2.0, None, ALU.add))
                link(nc.vector.reciprocal(r, d))
                link(nc.vector.tensor_tensor(z, e, r, ALU.mult))
                link(nc.vector.tensor_tensor(w, z, z, ALU.mult))
                link(nc.vector.tensor_scalar(q[0], w, ART[4], None, ALU.mult))
                for i, c in enumerate((ART[3], ART[2], ART[1])):
                    link(nc.vector.scalar_tensor_tensor(q[(i + 1) % 2], q[i % 2], c, w, ALU.add, ALU.mult))
                link(nc.vector.scalar_tensor_tensor(q[0], q[1], ART[0], z, ALU.add, ALU.mult))
                nc.vector.scalar_tensor_tensor(dt[:, p, :, :].rearrange("p k h -> p (k h)"),
                                               dx[:, p, :, :].rearrange("p k h -> p (k h)"), 0.0, q[0],
                                               ALU.max, ALU.add).then_inc(s_dt, 1)
                if p == 0:
                    dve.wait_ge(s_nega, 1)
                dve.wait_ge(s_dt, p + 1)
                nc.vector.tensor_tensor(a[:, p, :, :], dt[:, p, :, :],
                                        neg_a[:, :].unsqueeze(1).to_broadcast([128, K, NH]), ALU.mult)\
                    .then_inc(s_a, 1)

            def conv_silu(p):
                dve.wait_ge(s_half_t, p + 1)
                dve.wait_ge(s_half_v, p + 1)
                nc.vector.scalar_tensor_tensor(s[0:96, p, :, :], half_t[0:96, p, :, :], 1.0,
                                               half_v[0:96, p, :, :], ALU.add, ALU.mult).then_inc(s_s, 1)
                nc.vector.scalar_tensor_tensor(cs[64:96, p, :, :], half_t[96:128, p, :, :], 1.0,
                                               half_v[96:128, p, :, :], ALU.add, ALU.mult).then_inc(s_cs, 1)

            def gate_silu(p):
                dve.wait_ge(s_zt, p + 1)
                nc.vector.scalar_tensor_tensor(
                    zg[:, p, :, :], zt[:, p, :, :], 1.0,
                    ps_zdt[:, 0:K * ZD].rearrange("p (k z) -> p k z", k=K)[:, :, 0:C], ALU.add, ALU.mult)\
                    .then_inc(s_zg, 1)

            def token_inputs(p):
                dve.wait_ge(s_sT, p + 1)
                dve.wait_ge(s_dt, p + 1)
                tv = ps_sT[:, :].rearrange("p (k c) -> p k c", k=K)
                nc.vector.tensor_tensor(
                    dtx[:, p, :, :].rearrange("p k (h d) -> p k h d", h=NH),
                    tv[:, :, 0:C].rearrange("p k (h d) -> p k h d", h=NH),
                    dt[:, p, :, :].unsqueeze(3).to_broadcast([128, K, NH, HD]), ALU.mult).then_inc(s_dtx, 1)
                nc.vector.tensor_copy(bT[:, p, :, :], tv[:, 0:BP, C:C + DS]).then_inc(s_bT, 1)

            def mask_products(p):
                dve.wait_ge(s_G, p + 1)
                if p == 0:
                    dve.wait_ge(s_masks, 2)
                nc.vector.tensor_tensor(gm[:, p, :, :], ps_G[:, :].rearrange("p (k t) -> p k t", k=K),
                                        upto[:, :].unsqueeze(1).to_broadcast([128, K, T]), ALU.mult)\
                    .then_inc(s_gm, 1)
                dve.wait_ge(s_gm, p + 1)

            def weigh(p, k):
                dve.wait_ge(s_decay, K * p + k + 1)
                nc.vector.tensor_tensor(att[:, p, k, :, :], decay[:, p, k, :, :],
                                        gm[:, p, k, :].unsqueeze(1).to_broadcast([128, NH, T]), ALU.mult)\
                    .then_inc(s_att, 1)

            def state_inputs(p):
                dve.wait_ge(s_decay, K * p + BP)
                dve.wait_ge(s_dtx, p + 1)
                nc.vector.tensor_tensor(
                    wdtx[:, p, :, :].rearrange("p b (h d) -> p b h d", h=NH),
                    dtx[:, p, 0:BP, :].rearrange("p b (h d) -> p b h d", h=NH),
                    decay[:, p, 0:BP, :, T - 1:T].to_broadcast([128, BP, NH, HD]), ALU.mult)\
                    .then_inc(s_wdtx, 1)

            def gated(p):
                dve.wait_ge(s_inter, p + 1)
                dve.wait_ge(s_carry, p + 1)
                nc.vector.tensor_tensor(
                    yc[:, p, :, :].rearrange("p b (h d) -> p b h d", h=NH),
                    ps_mid[:, 128:256].rearrange("p (b h d) -> p b h d", b=BP, h=NH),
                    carry[:, p, :, :].unsqueeze(3).to_broadcast([128, BP, NH, HD]), ALU.mult).then_inc(s_yc, 1)
                dve.wait_ge(s_yc, p + 1)
                dve.wait_ge(s_ys, p + 1)
                dve.wait_ge(s_zg, p + 1)
                yv = ps_ys[:, 0:K * C].rearrange("p (k c) -> p k c", k=K)
                nc.vector.tensor_tensor(y2[:, p, 0:BP, :], yv[:, 0:BP, :], zg[:, p, 0:BP, :], ALU.mult)
                link(nc.vector.tensor_tensor(ys[:, p, :, :], yv[:, BP:K, :], yc[:, p, :, :], ALU.add))
                nc.vector.tensor_tensor(y2[:, p, BP:K, :], ys[:, p, :, :], zg[:, p, BP:K, :], ALU.mult)\
                    .then_inc(s_y2, 1)
                dve.wait_ge(s_y2, p + 1)
                link(nc.vector.tensor_tensor(ysq[:, p, :, :], y2[:, p, :, :], y2[:, p, :, :], ALU.mult))
                link(nc.vector.tensor_reduce(yss[:, p, :], ysq[:, p, :, :], AX.X, ALU.add))
                nc.vector.tensor_scalar(yve[:, p, :], yss[:, p, :], 1.0 / C, 4 * EPS, ALU.mult, ALU.add)\
                    .then_inc(s_yve, 1)

            def rms_scale(p):
                dve.wait_ge(s_yrs, p + 1)
                nc.vector.tensor_tensor(y3[:, p, :, :], y2[:, p, :, :],
                                        yrs[:, p, :].unsqueeze(2).to_broadcast([128, K, C]), ALU.mult)\
                    .then_inc(s_y3, 1)

            def finish(p):
                dve.wait_ge(s_gatet, p + 1)
                link(nc.vector.tensor_scalar(gate[:, p:p + 1], gate_t[:, p:p + 1], 0.5, 0.5, ALU.mult, ALU.add))
                dve.wait_ge(s_outp, p + 1)
                dve.wait_ge(s_hT, p + 1)
                nc.vector.scalar_tensor_tensor(res[:, p, :], ps_out[:, 256:512], gate[:, p:p + 1], hT[:, p, :],
                                               ALU.mult, ALU.add).then_inc(s_res, 1)

            weights()
            row_max(0, 0)
            row_max(0, 1)
            row_max(1, 0)
            probT_copy(0)
            row_max(1, 1)
            residual(0)
            layer_norm(0)
            layer_scale(0)
            probT_copy(1)
            layer_affine(0)
            dt_argument(0)
            residual(1)
            softplus(0)
            layer_norm(1)
            conv_silu(0)
            layer_scale(1)
            gate_silu(0)
            token_inputs(0)
            mask_products(0)
            layer_affine(1)
            dt_argument(1)
            for k in range(K):
                weigh(0, k)
                if k == BP - 1:
                    state_inputs(0)
            softplus(1)
            conv_silu(1)
            gate_silu(1)
            gated(0)
            token_inputs(1)
            mask_products(1)
            rms_scale(0)
            for k in range(K):
                weigh(1, k)
                if k == BP - 1:
                    state_inputs(1)
            finish(0)
            gated(1)
            rms_scale(1)
            finish(1)

        @block.tensor
        def _(pe):
            mm = nc.tensor.matmul

            pe.wait_ge(s_early, 16)

            mm(ps_setup[:, 0:C], pe_[0:C, E_WK:E_WK + 2 * C], pe_[0:C, E_WQ:E_WQ + C], start=True, stop=True)
            mm(ps_setup[:, C:2 * C], pe_[0:C, E_WV:E_WV + 2 * C], pe_[0:C, E_WPT:E_WPT + C],
               start=True, stop=True).then_inc(s_mixp, 1)
            pe.wait_ge(s_ident, 1)
            for p in range(PAIRS):
                pe.wait_ge(s_x[p], 16)
                for i in range(NT):
                    last = nc.tensor.transpose(ps_xT[:, (NT * p + i) * T:(NT * p + i + 1) * T],
                                               xc[:, p, T * i:T * i + T], ident[:, :])
                last.then_inc(s_xTp, 1)
            pe.wait_ge(s_group, 2)
            pe.wait_ge(s_gmq, 1)
            pe.wait_ge(s_mix, BP)
            mm(ps_setup[:, 128:128 + 2 * PAIRS], group_mean[:, :], gmq[:, :, :].rearrange("p m b -> p (m b)"),
               start=True, stop=True).then_inc(s_gg, 1)

            def project(p):
                pe.wait_ge(s_xn, p + 1)
                if p > 0:
                    pe.wait_ge(s_vals, p)
                mm(ps_proj[:, 0:N], mix[:, 0, :], xn[:, p, :], start=True, stop=True).then_inc(s_keysp, 1)
                pe.wait_ge(s_keys, p + 1)
                for i in range(NT):
                    last = mm(ps_proj[:, N + T * i:N + T * i + T], xn[:, p, T * i:T * i + T], mix[:, 1, :],
                              start=True, stop=True)
                last.then_inc(s_valsp, 1)

            def scores(p, b):
                pe.wait_ge(s_keys, p + 1)
                if p > 0:
                    pe.wait_ge(s_prob, NT * (b + 1))
                for i in range(NT):
                    mm(ps_score[b][:, N * i:N * i + N], xn[C * b:C * b + C, p, T * i:T * i + T],
                       keys[C * b:C * b + C, p, :], start=True, stop=True).then_inc(s_score, 1)

            def transpose_prob(p, b):
                if p > 0:
                    pe.wait_ge([s_probT0, s_probT1][b], p)
                for i in range(NT):
                    pe.wait_ge(s_prob, NT * (BP * p + b) + i + 1)
                    for j in range(NT):
                        last = nc.tensor.transpose(ps_probT[b][:, N * j + T * i:N * j + T * i + T],
                                                   prob[:, p, b, i, T * j:T * j + T], ident[:, :])
                last.then_inc(s_probTp, 1)

            def attend(p, b):
                if b == 0:
                    pe.wait_ge(s_vals, p + 1)
                    if p == 0:
                        pe.wait_ge(s_zero, 9)
                    else:
                        pe.wait_ge(s_hT, p)
                pe.wait_ge([s_probT0, s_probT1][b], p + 1)
                for i in range(NT):
                    k = BP * i + b
                    for j in range(NT):
                        last = mm(ps_y[:, (C + 1) * k:(C + 1) * (k + 1)], probT[:, p, b, j, T * i:T * i + T],
                                  vals[:, p, BP * j + b, :], start=(j == 0), stop=(j == NT - 1))
                if b == BP - 1:
                    last.then_inc(s_y, 1)

            def transpose_h(p):
                pe.wait_ge(s_h, p + 1)
                for i in range(NT):
                    last = nc.tensor.transpose(ps_y[:, T * i:T * i + T],
                                               h[:, p, BP * i:BP * i + BP, :].rearrange("p b c -> p (b c)"),
                                               ident[:, :])
                last.then_inc(s_hTp, 1)

            def weights():
                pe.wait_ge(s_convin, 1)
                pe.wait_ge(s_gve, 1)
                for j in range(2):
                    nc.tensor.transpose(ps_setup[:, T * j:T * j + T],
                                        conv_in[:, 2 * j:2 * j + 2, :].rearrange("p k c -> p (k c)"),
                                        ident[:, :])
                mm(ps_setup[:, 256:256 + HID], pl[0:C, L_OUTW:L_OUTW + 2 * C], pl[0:C, L_SE1T:L_SE1T + HID],
                   start=True, stop=True).then_inc(s_wconvp, 1)

            def transpose_u(p):
                if p == 0:
                    pe.wait_ge(s_xT, PAIRS)
                else:
                    pe.wait_ge(s_bT, p)
                for k in range(K):
                    i, b = divmod(k, BP)
                    pe.wait_ge(s_u, K * p + k + 1)
                    last = nc.tensor.transpose(ps_uT[:, N * b + T * i:N * b + T * i + T],
                                               u[:, p, k, :, :].rearrange("p j c -> p (j c)"),
                                               ident[:, :])
                last.then_inc(s_uTp, 1)

            def gate_dt(p):
                pe.wait_ge(s_uclo, p + 1)
                if p == 0:
                    pe.wait_ge(s_vals, PAIRS)
                else:
                    pe.wait_ge(s_zg, p)
                for k in range(K):
                    i, b = divmod(k, BP)
                    at = TAPS - 1 + T * i
                    last = mm(ps_zdt[:, ZD * k:ZD * k + ZD], uc[0:C, p, b, at:at + T],
                              pl[0:C, L_WZDT:L_WZDT + ZD], start=True, stop=True)
                last.then_inc(s_zdt, 1)

            def convolve(p):
                pe.wait_ge(s_uclo, p + 1)
                pe.wait_ge(s_uchi, p + 1)
                if p == 0:
                    pe.wait_ge(s_wconv, 1)
                    pe.wait_ge(s_se1, BP)
                else:
                    pe.wait_ge(s_gm, p)
                for j in range(2):
                    last = mm(ps_conv[:, :], conv_w[:, j, :], uc[:, p, :, 2 * j:2 * j + N],
                              start=(j == 0), stop=(j == 1))
                last.then_inc(s_conv, 1)

            def transpose_s(p):
                pe.wait_ge(s_s, p + 1)
                pe.wait_ge(s_uclo, p + 1)
                pe.wait_ge(s_uchi, p + 1)
                if p > 0:
                    pe.wait_ge(s_yc, p)
                for k in range(K):
                    i, b = divmod(k, BP)
                    last = nc.tensor.transpose(ps_sT[:, T * k:T * k + C + DS], s[0:C + DS, p, b, T * i:T * i + T],
                                               ident[0:C + DS, 0:C + DS])
                last.then_inc(s_sT, 1)

            def products(p):
                pe.wait_ge(s_cs, p + 1)
                for k in range(K):
                    i, b = divmod(k, BP)
                    last = mm(ps_G[:, T * k:T * k + T], s[C:C + DS, p, b, T * i:T * i + T],
                              cs[C:C + DS, p, b, T * i:T * i + T], start=True, stop=True)
                last.then_inc(s_G, 1)

            def segment_sums(p, k):
                if p == 0 and k == 0:
                    pe.wait_ge(s_masks, 1)
                    pe.wait_ge(s_prob, NT * B)
                    pe.wait_ge(s_probT0, PAIRS)
                    pe.wait_ge(s_probT1, PAIRS)
                if p > 0:
                    pe.wait_ge(s_decay, K * (p - 1) + k + 1)
                pe.wait_ge(s_am, K * p + k + 1)
                mm(ps_S[k][:, :], after[:, :], am[:, p, k, :, :].rearrange("p h t -> p (h t)"),
                   start=True, stop=True).then_inc(s_S, 1)

            def chunk_state(p):
                pe.wait_ge(s_bT, p + 1)
                pe.wait_ge(s_wdtx, p + 1)
                for b in range(BP):
                    mm(ps_mid[C:C + DS, C * b:C * b + C], bT[:, p, b, :], wdtx[:, p, b, :],
                       start=True, stop=True)
                if p == 0:
                    pe.wait_ge(s_masks, 2)
                mm(ps_mid[:, 256:256 + BP * NH], upto[:, :], a[:, p, BP:K, :].rearrange("p b h -> p (b h)"),
                   start=True, stop=True).then_inc(s_statep, 1)

            def carried(p):
                pe.wait_ge(s_state, p + 1)
                pe.wait_ge(s_carry, p + 1)
                for b in range(BP):
                    last = mm(ps_mid[:, 128 + C * b:128 + C * b + C], cs[C:C + DS, p, b, T:2 * T],
                              state[C:C + DS, p, b, :], start=True, stop=True)
                last.then_inc(s_inter, 1)

            def chunk_output(p, k):
                i, b = divmod(k, BP)
                if k == 0:
                    if p == 0:
                        pe.wait_ge(s_diag, 1)
                        pe.wait_ge(s_hT, PAIRS)
                    else:
                        pe.wait_ge(s_y2, p)
                    pe.wait_ge(s_dtx, p + 1)
                mm(ps_ys[:, C * k:C * k + C], s[0:C, p, b, T * i:T * i + T], diag_d[:, :],
                   start=True, stop=False)
                pe.wait_ge(s_att, K * p + k + 1)
                for hd in range(NH):
                    last = mm(ps_ys[:, C * k + HD * hd:C * k + HD * hd + HD], att[:, p, k, hd, :],
                              dtx[:, p, k, HD * hd:HD * hd + HD], start=False, stop=(hd == NH - 1))
                if k == K - 1:
                    last.then_inc(s_ys, 1)

            def transpose_y3(p):
                pe.wait_ge(s_y3, p + 1)
                pe.wait_ge(s_gm, min(p + 2, PAIRS))
                if p > 0:
                    pe.wait_ge(s_res, p)
                for i in range(NT):
                    last = nc.tensor.transpose(ps_y3T[:, T * i:T * i + T],
                                               y3[:, p, BP * i:BP * i + BP, :].rearrange("p b c -> p (b c)"),
                                               ident[:, :])
                last.then_inc(s_y3Tp, 1)

            def out_project(p):
                pe.wait_ge(s_y3T, p + 1)
                if p == 0:
                    pe.wait_ge(s_zg, PAIRS)
                else:
                    pe.wait_ge(s_gatet, p)
                mm(ps_se[0:BP * HID, 0:1], se1[:, :], ysum[:, p:p + 1], start=True, stop=True)\
                    .then_inc(s_hidp, 1)
                mm(ps_out[:, 256:512], pl[:, L_OUTWT:L_OUTWT + 128], y3T[:, p, :], start=True, stop=True)\
                    .then_inc(s_outp, 1)
                pe.wait_ge(s_hid, p + 1)
                mm(ps_se[:, 1:2], pl[0:BP * HID, L_SE2T:L_SE2T + 128], hidden[:, p:p + 1],
                   start=True, stop=True).then_inc(s_gatep, 1)

            project(0)
            scores(0, 0)
            scores(0, 1)
            project(1)
            weights()
            transpose_prob(0, 0)
            scores(1, 0)
            transpose_prob(0, 1)
            scores(1, 1)
            attend(0, 0)
            attend(0, 1)
            transpose_prob(1, 0)
            transpose_prob(1, 1)
            transpose_h(0)
            transpose_u(0)
            attend(1, 0)
            attend(1, 1)
            gate_dt(0)
            convolve(0)
            transpose_h(1)
            transpose_s(0)
            products(0)
            transpose_u(1)
            for k in range(K):
                segment_sums(0, k)
            gate_dt(1)
            convolve(1)
            for k in range(K):
                chunk_output(0, k)
            chunk_state(0)
            carried(0)
            transpose_s(1)
            products(1)
            for k in range(K):
                segment_sums(1, k)
            transpose_y3(0)
            for k in range(BP):
                chunk_output(1, k)
            out_project(0)
            for k in range(BP, K):
                chunk_output(1, k)
            chunk_state(1)
            carried(1)
            transpose_y3(1)
            out_project(1)


def kernel(**inputs):
    import numpy as np
    import concourse.bacc as bacc
    from concourse.bass_utils import run_bass_kernel_spmd

    f = {name: np.asarray(value) for name, value in inputs.items()}

    def column(v, rows=128):
        col = np.zeros((128, 1), np.float32)
        col[:rows, 0] = np.concatenate([v] * (rows // v.shape[0]))
        return col

    def row(v):
        return np.ascontiguousarray(np.broadcast_to(v[None, :], (128, v.shape[0])))

    def top(m):
        full = np.zeros((128, m.shape[1]), np.float32)
        full[:m.shape[0]] = m
        return full

    def twice(m):
        return np.concatenate([m, m], axis=1)

    def diagonal(m):
        r, c = m.shape
        full = np.zeros((128, BP * c), np.float32)
        for b in range(BP):
            full[r * b:r * b + r, c * b:c * b + c] = m
        return full

    w = f["L0_conv_w_qkv"]
    early = np.concatenate([
        column(f["L0_conv_gamma"]), column(f["L0_conv_beta"]),
        top(w[0:C]), top(twice(w[C:2 * C])), top(twice(w[2 * C:3 * C])), top(f["L0_conv_w_proj"].T),
        row(f["L0_conv_b_proj"])], axis=1)
    inw = f["L1_conv_in_w"]
    xbc = inw[C:C + 128]
    zdt = np.concatenate([inw[0:C], inw[C + 128:]], axis=0)
    late = np.concatenate([
        column(f["L1_conv_norm_g"]), column(f["L1_conv_norm_b"]), column(f["L1_conv_rms_w"]),
        column(np.repeat(f["L1_conv_Dp"], HD)), column(f["L1_conv_conv_b"]), column(f["L1_conv_se2_b"]),
        column(f["L1_conv_se1_b"], BP * HID), np.zeros((128, 1), np.float32),
        f["L1_conv_conv_w"], row(f["L1_conv_dt_bias"]), row(f["L1_conv_A_log"]),
        xbc, top(zdt.T), top(twice(f["L1_conv_out_w"])), diagonal(f["L1_conv_out_w"].T),
        top(f["L1_conv_se1_w"].T), diagonal(f["L1_conv_se2_w"].T)], axis=1)

    fp32 = mybir.dt.float32
    nc = bacc.Bacc("TRN2", target_bir_lowering=False, num_devices=1)
    arrays = {"in_x": np.ascontiguousarray(f["x"]), "in_early": early, "in_late": late}
    args = [nc.dram_tensor(n, v.shape, fp32, kind="ExternalInput").ap() for n, v in arrays.items()]
    args.append(nc.dram_tensor("out_0", f["x"].shape, fp32, kind="ExternalOutput").ap())
    attention_mamba_kernel(nc, *args)
    r = run_bass_kernel_spmd(nc, [arrays], core_ids=[0])
    return r.results[0]["out_0"]
```

```python
import concourse.bass as bass
from concourse import mybir
from contextlib import ExitStack
import math

B, C, N = 4, 64, 256
BP = 2
PAIRS = B // BP
T = 128
NT = N // T
K = NT * BP
GROUP = C // 8
NH, HD, DS = 4, 16, 32
TAPS = 4
HID = C // 4
OC = C + HID
UP = N + TAPS
EPS = 1e-5
SOFTPLUS = 11
WARM = {
    ("start", 0): 3584,
    ("group", 0): 2560,
    ("transpose_prob", 0, 0): 512,
    ("transpose_u", 0): 512,
    ("project_dt", 0): 512,
    ("transpose_s", 0): 1024,
    ("project_dt", 1): 512,
    ("transpose_s", 1): 1024,
}

E_GAMMA, E_BETA, E_WQ, E_WK, E_WV, E_WPT, E_BPROJ = 0, 1, 2, 66, 194, 322, 386
E_COLS = 450
L_NG, L_NB, L_RMS, L_D, L_CONVB, L_SE2B, L_SE1B = 0, 1, 2, 3, 4, 5, 6
L_CONVW, L_DTB, L_ALOG, L_INW, L_WZ, L_WDT = 8, 12, 16, 20, 84, 148
L_OUTW, L_OUTWT, L_SE1T, L_SE2T = 152, 280, 344, 360
L_PICK = 488
L_COLS = 490


def artanh_coefficients(degree):
    import numpy as np
    k = np.arange(64)
    w = (1 + np.cos(np.pi * (k + 0.5) / 64)) / 18
    z = np.sqrt(w)
    fit = np.polynomial.chebyshev.Chebyshev.fit(w, 2 * np.arctanh(z) / z, degree, domain=[0, 1 / 9])
    return [float(c) for c in fit.convert(kind=np.polynomial.Polynomial).coef]


def attention_mamba_kernel(nc: bass.Bass, x: bass.AP, early: bass.AP, late: bass.AP, out: bass.AP):
    fp32 = mybir.dt.float32
    ALU = mybir.AluOpType
    ACT = mybir.ActivationFunctionType
    AX = mybir.AxisListType
    ART = artanh_coefficients(4)

    x_v = x.rearrange("(p b) c h w -> p (b c) (h w)", b=BP)
    out_v = out.rearrange("(p b) c h w -> p (b c) (h w)", b=BP)

    ctx = ExitStack()
    with ctx:
        def sb(name, shape):
            return ctx.enter_context(nc.sbuf_tensor(name, shape, fp32))

        busy = ctx.enter_context(nc.sbuf_tensor("busy", [128, 512], mybir.dt.bfloat16))

        def sem(name):
            return ctx.enter_context(nc.semaphore(name))

        xc = sb("xc", [128, PAIRS, N])
        pe_ = sb("params_early", [128, E_COLS])
        pl = sb("params_late", [128, L_COLS])
        ident = sb("ident", [128, 128])
        group_mean = sb("group_mean", [128, 128])
        after = sb("after", [128, 128])
        upto = sb("upto", [128, 128])
        minus_half = sb("minus_half", [128, 4])

        mix = sb("mix", [128, 2, 128])
        conv_in = sb("conv_in", [128, TAPS, C])
        conv_w = sb("conv_w", [128, 2, 128])
        diag_d = sb("diag_d", [128, C])
        outw = sb("outw", [128, BP, OC])
        ones = sb("ones", [128, 1])
        neg_a = sb("neg_a", [128, NH])
        half_bias = sb("half_bias", [128, 2])
        half_rms = sb("half_rms", [128, 1])

        gst = sb("gst", [128, PAIRS, 6])
        gmv = sb("gmv", [128, PAIRS, 2])
        gsq = sb("gsq", [128, PAIRS])
        gg = sb("gg", [128, PAIRS, 2])
        ggsq = sb("ggsq", [128, PAIRS])
        gve = sb("gve", [128, PAIRS])
        grs = sb("grs", [128, PAIRS])
        gscale = sb("gscale", [128, PAIRS])
        xm = sb("xm", [128, PAIRS, N])
        xn = sb("xn", [128, PAIRS, N])

        keys = sb("keys", [128, PAIRS, BP, N])
        vals = sb("vals", [128, PAIRS, K, C + 1])
        xT = sb("xT", [128, PAIRS, K, C])
        neg_max = sb("neg_max", [128, PAIRS, BP, NT])
        prob = sb("prob", [128, PAIRS, BP, NT, N])
        probT = sb("probT", [128, PAIRS, BP, NT, N])
        rden = sb("rden", [128, PAIRS, K])
        ynorm = sb("ynorm", [128, PAIRS, K, C])
        h = sb("h", [128, PAIRS, K, C])
        hT = sb("hT", [128, PAIRS, N])

        lst = sb("lst", [128, PAIRS, K, 6])
        lmv = sb("lmv", [128, PAIRS, K, 2])
        lve = sb("lve", [128, PAIRS, K])
        lrs = sb("lrs", [128, PAIRS, K])
        u = sb("u", [128, PAIRS, K, 2, C])
        uc = sb("uc", [128, PAIRS, BP, UP])
        half_v = sb("half_v", [128, PAIRS, BP, N])
        half_t = sb("half_t", [128, PAIRS, BP, N])
        s = sb("s", [128, PAIRS, BP, N])
        cs = sb("cs", [128, PAIRS, BP, N])
        zt = sb("zt", [128, PAIRS, N])
        zg = sb("zg", [128, PAIRS, N])

        dx = sb("dx", [128, PAIRS, K, NH])
        dn = sb("dn", [128, PAIRS, K * NH])
        de = sb("de", [128, PAIRS, K * NH])
        dd = sb("dd", [128, PAIRS, K * NH])
        dr = sb("dr", [128, PAIRS, K * NH])
        dz = sb("dz", [128, PAIRS, K * NH])
        dw = sb("dw", [128, PAIRS, K * NH])
        dq = sb("dq", [128, PAIRS, 2, K * NH])
        dt = sb("dt", [128, PAIRS, K, NH])
        a = sb("a", [128, PAIRS, K, NH])

        am = sb("am", [128, PAIRS, K, NH, T])
        decay = sb("decay", [128, PAIRS, K, NH, T])
        gm = sb("gm", [128, PAIRS, K, T])
        att = sb("att", [128, PAIRS, K, NH, T])
        dtx = sb("dtx", [128, PAIRS, K, NH, C])
        bT = sb("bT", [128, PAIRS, BP, DS])
        wdtx = sb("wdtx", [128, PAIRS, BP, C])
        state = sb("state", [128, PAIRS, BP, C])
        a_wide = sb("a_wide", [128, PAIRS, BP, NH, HD])
        carry = sb("carry", [128, PAIRS, T])
        yc = sb("yc", [128, PAIRS, T])
        ys = sb("ys", [128, PAIRS, T])

        y2 = sb("y2", [128, PAIRS, N])
        ysq = sb("ysq", [128, PAIRS, N])
        yve = sb("yve", [128, PAIRS, K])
        yrs = sb("yrs", [128, PAIRS, K])
        o3 = sb("o3", [128, PAIRS, NT, BP * C])
        q3 = sb("q3", [128, PAIRS, NT, BP * HID])
        hidden = sb("hidden", [BP * HID, PAIRS])
        gate_t = sb("gate_t", [128, PAIRS])
        base = sb("base", [128, PAIRS, N])
        res = sb("res", [128, PAIRS, N])

        bank = [ctx.enter_context(nc.psum_tensor(f"bank{i}", [128, 512], fp32)) for i in range(8)]
        ps_setup = bank[7]
        ps_group = bank[5]
        ps_xT = bank[6]
        ps_keys = bank[0]
        ps_vals = bank[5]
        ps_score = [bank[1], bank[2]]
        ps_probT = [bank[3], bank[4]]
        ps_y = bank[5]
        ps_uT = bank[6]
        ps_conv = bank[7]
        ps_dt = bank[0]
        ps_z = bank[0]
        ps_sT = bank[6]
        ps_G = bank[7]
        ps_S = [bank[1], bank[2], bank[3]]
        ps_ys = [bank[5], bank[4]]
        ps_mid = bank[6]
        ps_o = [bank[5], bank[4]]
        ps_out = bank[7]
        ps_se = bank[0]

        s_x = [sem(f"s_x{p}") for p in range(PAIRS)]
        s_early, s_late, s_out = sem("s_early"), sem("s_late"), sem("s_out")
        s_zero, s_ident, s_group, s_masks = sem("s_zero"), sem("s_ident"), sem("s_group"), sem("s_masks")
        s_mixp, s_mix = sem("s_mixp"), sem("s_mix")
        s_gsq, s_gg, s_gve, s_grs = sem("s_gsq"), sem("s_gg"), sem("s_gve"), sem("s_grs")
        s_gread, s_gscale, s_xm, s_xn0, s_xn1 = (sem("s_gread"), sem("s_gscale"), sem("s_xm"), sem("s_xn0"),
                                                 sem("s_xn1"))
        s_busy, s_pad = sem("s_busy"), sem("s_pad")
        s_xTp, s_xT = sem("s_xTp"), sem("s_xT")
        s_keysp, s_valsp, s_keys, s_vals = sem("s_keysp"), sem("s_valsp"), sem("s_keys"), sem("s_vals")
        s_score, s_max, s_prob, s_probTp = sem("s_score"), sem("s_max"), sem("s_prob"), sem("s_probTp")
        s_probT = sem("s_probT")
        s_y, s_yread, s_h, s_hTp, s_hT = sem("s_y"), sem("s_yread"), sem("s_h"), sem("s_hTp"), sem("s_hT")
        s_lve, s_lrs, s_u, s_uTp = sem("s_lve"), sem("s_lrs"), sem("s_u"), sem("s_uTp")
        s_upool = sem("s_upool")
        s_uclo, s_uchi = sem("s_uclo"), sem("s_uchi")
        s_convin, s_wconvp, s_wconv, s_se1p, s_outw = (sem("s_convin"), sem("s_wconvp"), sem("s_wconv"),
                                                      sem("s_se1p"), sem("s_outw"))
        s_aexp, s_nega, s_diag, s_half = sem("s_aexp"), sem("s_nega"), sem("s_diag"), sem("s_half")
        s_conv, s_half_v, s_half_t, s_s, s_cs = (sem("s_conv"), sem("s_half_v"), sem("s_half_t"),
                                                 sem("s_s"), sem("s_cs"))
        s_dtp, s_zp, s_zt, s_zg, s_dx = sem("s_dtp"), sem("s_zp"), sem("s_zt"), sem("s_zg"), sem("s_dx")
        s_dn, s_de, s_softplus = sem("s_dn"), sem("s_de"), sem("s_softplus")
        s_am, s_S, s_decay = sem("s_am"), sem("s_S"), sem("s_decay")
        s_sT, s_dtx, s_bT, s_G, s_gm, s_att = (sem("s_sT"), sem("s_dtx"), sem("s_bT"), sem("s_G"),
                                               sem("s_gm"), sem("s_att"))
        s_wdtx, s_statep, s_state, s_awide, s_carry = (sem("s_wdtx"), sem("s_statep"), sem("s_state"),
                                                       sem("s_awide"), sem("s_carry"))
        s_inter, s_ys, s_yc, s_y2, s_ysq = sem("s_inter"), sem("s_ys"), sem("s_yc"), sem("s_y2"), sem("s_ysq")
        s_o, s_yve, s_yrs, s_o3, s_outp = sem("s_o"), sem("s_yve"), sem("s_yrs"), sem("s_o3"), sem("s_outp")
        s_hidp, s_hid, s_gatep, s_gatet = sem("s_hidp"), sem("s_hid"), sem("s_gatep"), sem("s_gatet")
        s_res = sem("s_res")
        s_vec, s_act = sem("s_vec"), sem("s_act")
        s_bn = sem("s_bn")

        block = ctx.enter_context(nc.Block())

        @block.sync
        def _(sync):
            sync.dma_start(xc[:, 0, :], x_v[0]).then_inc(s_x[0], 16)
            sync.dma_start(pe_[:, :], early).then_inc(s_early, 16)
            for p in range(PAIRS):
                sync.wait_ge(s_res, p + 1)
                sync.dma_start(out_v[p], res[:, p, :]).then_inc(s_out, 16)
            sync.wait_ge(s_out, 16 * PAIRS)

        @block.gpsimd
        def _(pool):
            def mark(ap, value, keep, compare, base, pattern, channel):
                return nc.gpsimd.affine_select(out=ap, in_=ap, compare_op=compare, fill=value, base=base,
                                               pattern=pattern, channel_multiplier=channel)

            nc.gpsimd.memset(busy[:, :], 0.0).then_inc(s_busy, 1)
            nc.gpsimd.memset(group_mean[:, :], 1.0 / GROUP).then_inc(s_zero, 1)
            nc.gpsimd.memset(ident[:, :], 0.0).then_inc(s_zero, 1)
            nc.gpsimd.memset(minus_half[:, :], -0.5).then_inc(s_zero, 1)
            nc.gpsimd.memset(mix[:, :, :], 0.0).then_inc(s_zero, 1)
            pool.wait_ge(s_zero, 4)
            gv = group_mean[:, :].rearrange("c (g j) -> c g j", j=GROUP)
            gpat = [[-GROUP, 128 // GROUP], [0, GROUP]]
            mark(gv, 0.0, True, ALU.is_ge, 0, gpat, 1).then_inc(s_group, 1)
            pool.wait_ge(s_group, 1)
            nc.gpsimd.affine_select(out=gv, in_=gv, compare_op=ALU.is_ge, fill=0.0, base=GROUP - 1,
                                    pattern=[[GROUP, 128 // GROUP], [0, GROUP]],
                                    channel_multiplier=-1).then_inc(s_group, 1)
            nc.gpsimd.affine_select(out=ident[:, :], in_=ident[:, :], compare_op=ALU.not_equal, fill=1.0,
                                    base=0, pattern=[[-1, 128]], channel_multiplier=1).then_inc(s_ident, 1)
            nc.gpsimd.memset(keys[:, :, :, :], 0.0).then_inc(s_pad, 1)
            nc.gpsimd.memset(after[:, :], 1.0).then_inc(s_zero, 1)
            nc.gpsimd.memset(upto[:, :], 1.0).then_inc(s_zero, 1)
            nc.gpsimd.memset(outw[:, :, :], 0.0).then_inc(s_zero, 1)
            nc.gpsimd.memset(uc[:, :, :, :], 0.0).then_inc(s_zero, 1)
            nc.gpsimd.memset(vals[:, :, :, C:C + 1], 1.0).then_inc(s_zero, 1)
            pool.wait_ge(s_zero, 9)
            nc.gpsimd.affine_select(out=after[:, :], in_=after[:, :], compare_op=ALU.is_gt, fill=0.0, base=0,
                                    pattern=[[-1, 128]], channel_multiplier=1).then_inc(s_masks, 1)
            nc.gpsimd.affine_select(out=upto[:, :], in_=upto[:, :], compare_op=ALU.is_ge, fill=0.0, base=0,
                                    pattern=[[1, 128]], channel_multiplier=-1).then_inc(s_masks, 1)
            pool.wait_ge(s_gve, 1)
            nc.gpsimd.tensor_tensor(grs[:, :], gve[:, :], minus_half[:, 0:PAIRS], ALU.pow).then_inc(s_grs, 1)

            nc.gpsimd.memset(cs[:, :, :, :], 0.0).then_inc(s_pad, 1)
            nc.gpsimd.memset(state[:, :, :, :], 0.0).then_inc(s_pad, 1)
            nc.gpsimd.memset(ones[:, :], 1.0).then_inc(s_pad, 1)
            nc.gpsimd.memset(dtx[:, :, :, :, :], 0.0).then_inc(s_pad, 1)

            def layer_rstd(p):
                pool.wait_ge(s_lve, p + 1)
                nc.gpsimd.tensor_tensor(lrs[:, p, :], lve[:, p, :], minus_half[:, 0:K], ALU.pow)\
                    .then_inc(s_lrs, 1)
                pool.wait_ge(s_lrs, p + 1)
                for k in range(BP, K):
                    nc.gpsimd.tensor_scalar(u[:, p, k, :, :],
                                            h[:, p, k, :].unsqueeze(1).to_broadcast([128, 2, C]), lmv[:, p, k, 0:1],
                                            lrs[:, p, k:k + 1], ALU.subtract, ALU.mult).then_inc(s_upool, 1)

            def masked_decay(p):
                pool.wait_ge(s_softplus, SOFTPLUS * (p + 1))
                for k in range(K):
                    nc.gpsimd.affine_select(
                        out=am[:, p, k, :, :], in_=a[:, p, k, :].unsqueeze(2).to_broadcast([128, NH, T]),
                        compare_op=ALU.is_ge, fill=0.0, base=0, pattern=[[0, NH], [1, T]],
                        channel_multiplier=-1).then_inc(s_am, 1)
                nc.gpsimd.tensor_copy(a_wide[:, p, :, :, :],
                                      a[:, p, BP:K, :].unsqueeze(3).to_broadcast([128, BP, NH, HD]))\
                    .then_inc(s_awide, 1)

            def rms_rstd(p, i):
                pool.wait_ge(s_yve, NT * p + i + 1)
                nc.gpsimd.tensor_tensor(yrs[:, p, BP * i:BP * i + BP], yve[:, p, BP * i:BP * i + BP],
                                        minus_half[:, 0:BP], ALU.pow).then_inc(s_yrs, 1)

            layer_rstd(0)
            layer_rstd(1)
            masked_decay(0)
            rms_rstd(0, 0)
            rms_rstd(0, 1)
            masked_decay(1)
            rms_rstd(1, 0)
            rms_rstd(1, 1)

        @block.scalar
        def _(act):
            done = [0]

            def link(ins):
                done[0] += 1
                ins.then_inc(s_act, 1)
                act.wait_ge(s_act, done[0])

            act.dma_start(xc[:, 1, :], x_v[1]).then_inc(s_x[1], 16)
            act.dma_start(pl[:, :], late).then_inc(s_late, 16)

            act.wait_ge(s_mixp, 1)
            act.wait_ge(s_zero, 4)
            mp = ps_setup[:, 0:2 * C].rearrange("p (m c) -> p m c", m=2)
            for b in range(BP):
                nc.scalar.activation(mix[C * b:C * b + C, :, C * b:C * b + C], mp[C * b:C * b + C, :, :],
                                     ACT.Copy).then_inc(s_mix, 1)
            act.wait_ge(s_late, 16)
            link(nc.scalar.activation(neg_a[:, :], pl[:, L_ALOG:L_ALOG + NH], ACT.Exp))
            nc.scalar.mul(neg_a[:, :], neg_a[:, :], -1.0).then_inc(s_nega, 1)
            nc.scalar.mul(half_bias[:, :], pl[:, L_CONVB:L_CONVB + 2], 0.5).then_inc(s_half, 1)
            nc.scalar.mul(half_rms[:, :], pl[:, L_RMS:L_RMS + 1], 0.5).then_inc(s_half, 1)

            def group_norm(p):
                act.wait_ge(s_gscale, 1)
                act.wait_ge(s_xm, 1)
                nc.scalar.activation(xn[:, p, :], xm[:, p, :], ACT.Identity, scale=gscale[:, p:p + 1],
                                     bias=pe_[:, E_BETA:E_BETA + 1]).then_inc(s_xn1, 1)

            def keys_copy(p):
                act.wait_ge(s_keysp, p + 1)
                if p == 0:
                    act.wait_ge(s_pad, 1)
                for b in range(BP):
                    rows = slice(C * b, C * b + C)
                    nc.scalar.activation(keys[rows, p, b, :], ps_keys[rows, 0:N], ACT.Copy, scale=C ** -0.5)\
                        .then_inc(s_keys, 1)

            def values_copy(p):
                act.wait_ge(s_valsp, p + 1)
                nc.scalar.activation(vals[:, p, :, 0:C],
                                     ps_vals[:, 0:N].rearrange("p (k c) -> p k c", k=K), ACT.Copy)\
                    .then_inc(s_vals, 1)

            def softmax(p, b):
                act.wait_ge(s_max, BP * p + b + 1)
                for i in range(NT):
                    nc.scalar.activation(prob[:, p, b, i, :], ps_score[b][:, N * i:N * i + N], ACT.Exp,
                                         bias=neg_max[:, p, b, i:i + 1]).then_inc(s_prob, 1)

            def probT_copy(p, b):
                act.wait_ge(s_probTp, BP * p + b + 1)
                nc.scalar.activation(probT[:, p, b, :, :].rearrange("p i n -> p (i n)"), ps_probT[b][:, :],
                                     ACT.Copy).then_inc(s_probT, 1)

            def h_copy(p):
                act.wait_ge(s_hTp, p + 1)
                nc.scalar.activation(hT[:, p, :], ps_y[:, 0:N], ACT.Copy).then_inc(s_hT, 1)

            def layer_affine(p):
                if p == 0:
                    act.wait_ge(s_zero, 8)
                act.wait_ge(s_uTp, p + 1)
                nc.scalar.activation(uc[0:C, p, :, TAPS - 1:TAPS - 1 + N],
                                     ps_uT[0:C, :].rearrange("p (b n) -> p b n", b=BP), ACT.Identity,
                                     scale=pl[0:C, L_NG:L_NG + 1], bias=pl[0:C, L_NB:L_NB + 1])\
                    .then_inc(s_uclo, 1)

            def gate_tanh(p):
                act.wait_ge(s_zp, p + 1)
                nc.scalar.activation(zt[:, p, :], ps_z[:, N:2 * N], ACT.Tanh, scale=0.5).then_inc(s_zt, 1)

            def conv_silu(p):
                if p == 0:
                    act.wait_ge(s_half, 2)
                act.wait_ge(s_conv, p + 1)
                cv = ps_conv[:, :]
                nc.scalar.activation(half_t[:, p, :, :].rearrange("p b n -> p (b n)"), cv, ACT.Tanh,
                                     scale=0.5, bias=half_bias[:, 0:1]).then_inc(s_half_t, 1)
                nc.scalar.activation(half_v[:, p, :, :].rearrange("p b n -> p (b n)"), cv, ACT.Identity,
                                     scale=0.5, bias=half_bias[:, 0:1]).then_inc(s_half_v, 1)

            def c_copy(p):
                if p == 0:
                    act.wait_ge(s_pad, 3)
                act.wait_ge(s_s, p + 1)
                nc.scalar.activation(cs[C:C + DS, p, :, :], s[C + DS:C + 2 * DS, p, :, :], ACT.Copy)\
                    .then_inc(s_cs, 1)

            def dt_exp(p):
                act.wait_ge(s_dn, p + 1)
                nc.scalar.activation(de[:, p, :], dn[:, p, :], ACT.Exp).then_inc(s_de, 1)

            def decays(p, k):
                act.wait_ge(s_S, K * p + k + 1)
                nc.scalar.activation(decay[:, p, k, :, :].rearrange("p h t -> p (h t)"),
                                     ps_S[(K * p + k) % len(ps_S)][:, :],
                                     ACT.Exp).then_inc(s_decay, 1)

            def chunk_state(p):
                if p == 0:
                    act.wait_ge(s_pad, 3)
                act.wait_ge(s_statep, p + 1)
                nc.scalar.activation(state[C:C + DS, p, :, :].rearrange("p b c -> p (b c)"),
                                     ps_mid[C:C + DS, 0:BP * C], ACT.Copy).then_inc(s_state, 1)
                nc.scalar.activation(carry[:, p, :], ps_mid[:, 256:256 + T], ACT.Exp).then_inc(s_carry, 1)

            def square(p, i):
                act.wait_ge(s_y2, NT * p + i + 1)
                nc.scalar.activation(ysq[:, p, T * i:T * i + T], y2[:, p, T * i:T * i + T], ACT.Square)\
                    .then_inc(s_ysq, 1)

            def squeeze(p):
                act.wait_ge(s_hidp, p + 1)
                nc.scalar.activation(hidden[:, p:p + 1], ps_se[0:BP * HID, 0:1], ACT.Relu, scale=2.0 / N,
                                     bias=pl[0:BP * HID, L_SE1B:L_SE1B + 1]).then_inc(s_hid, 1)
                act.wait_ge(s_gatep, p + 1)
                nc.scalar.activation(gate_t[:, p:p + 1], ps_se[:, 1:2], ACT.Tanh, scale=0.5,
                                     bias=half_bias[:, 1:2]).then_inc(s_gatet, 1)

            group_norm(1)
            keys_copy(0)
            values_copy(0)
            keys_copy(1)
            values_copy(1)
            softmax(0, 0)
            softmax(0, 1)
            probT_copy(0, 0)
            probT_copy(0, 1)
            softmax(1, 0)
            softmax(1, 1)
            h_copy(0)
            probT_copy(1, 0)
            probT_copy(1, 1)
            layer_affine(0)
            dt_exp(0)
            conv_silu(0)
            c_copy(0)
            gate_tanh(0)
            h_copy(1)
            layer_affine(1)
            decays(0, 0)
            decays(0, 1)
            decays(0, 2)
            decays(0, 3)
            dt_exp(1)
            conv_silu(1)
            c_copy(1)
            gate_tanh(1)
            chunk_state(0)
            square(0, 0)
            square(0, 1)
            decays(1, 0)
            decays(1, 1)
            decays(1, 2)
            decays(1, 3)
            squeeze(0)
            chunk_state(1)
            square(1, 0)
            square(1, 1)
            squeeze(1)

        @block.vector
        def _(dve):
            done = [0]

            def link(ins):
                done[0] += 1
                ins.then_inc(s_vec, 1)
                dve.wait_ge(s_vec, done[0])

            for p in range(PAIRS):
                dve.wait_ge(s_x[p], 16)
                nc.vector.bn_stats(gst[:, p, :], xc[:, p, :]).then_inc(s_vec, 1)
                done[0] += 1
            for p in range(PAIRS):
                dve.wait_ge(s_vec, p + 1)
                last = nc.vector.bn_aggr(gmv[:, p, :], gst[:, p, :])
                last.then_inc(s_vec, 1)
                done[0] += 1
            dve.wait_ge(s_vec, done[0])
            nc.vector.tensor_tensor(gsq[:, :], gmv[:, :, 0], gmv[:, :, 0], ALU.mult).then_inc(s_gsq, 1)
            dve.wait_ge(s_gg, 1)
            nc.vector.tensor_copy(gg[:, :, :].rearrange("p b m -> p (b m)"), ps_group[:, 0:2 * PAIRS])\
                .then_inc(s_gread, 1)
            dve.wait_ge(s_gread, 1)
            link(nc.vector.tensor_tensor(ggsq[:, :], gg[:, :, 0], gg[:, :, 0], ALU.mult))
            nc.vector.scalar_tensor_tensor(gve[:, :], gg[:, :, 1], EPS, ggsq[:, :], ALU.add, ALU.subtract)\
                .then_inc(s_gve, 1)
            for p in (1, 0):
                nc.vector.tensor_scalar(xm[:, p, :], xc[:, p, :], gg[:, p, 0:1], None, ALU.subtract)\
                    .then_inc(s_xm, 1)
            dve.wait_ge(s_early, 16)
            dve.wait_ge(s_grs, 1)
            nc.vector.tensor_scalar(gscale[:, :], grs[:, :], pe_[:, E_GAMMA:E_GAMMA + 1], None, ALU.mult)\
                .then_inc(s_gscale, 1)
            dve.wait_ge(s_gscale, 1)
            dve.wait_ge(s_xm, 2)
            nc.vector.tensor_scalar(xn[:, 0, :], xm[:, 0, :], gscale[:, 0:1], pe_[:, E_BETA:E_BETA + 1],
                                    ALU.mult, ALU.add).then_inc(s_xn0, 1)

            def tokens(p):
                dve.wait_ge(s_xTp, PAIRS)
                nc.vector.tensor_tensor(
                    xT[:, p, :, :], ps_xT[:, N * p:N * p + N].rearrange("p (k c) -> p k c", k=K),
                    pe_[:, E_BPROJ:E_BPROJ + C].unsqueeze(1).to_broadcast([128, K, C]), ALU.add)\
                    .then_inc(s_xT, 1)

            def row_max(p, b):
                dve.wait_ge(s_score, NT * (BP * p + b) + NT)
                nc.vector.tensor_reduce(neg_max[:, p, b, :], ps_score[b][:, :].rearrange("p (i m) -> p i m", i=NT),
                                        AX.X, ALU.max, negate=True).then_inc(s_max, 1)

            def residual(p):
                dve.wait_ge(s_y, p + 1)
                yv = ps_y[:, 0:K * (C + 1)].rearrange("p (k c) -> p k c", k=K)
                link(nc.vector.reciprocal(rden[:, p, :], yv[:, :, C]))
                nc.vector.tensor_tensor(ynorm[:, p, :, :], yv[:, :, 0:C],
                                        rden[:, p, :].unsqueeze(2).to_broadcast([128, K, C]), ALU.mult)\
                    .then_inc(s_yread, 1)
                dve.wait_ge(s_yread, p + 1)
                dve.wait_ge(s_xT, PAIRS)
                nc.vector.tensor_tensor(h[:, p, :, :], ynorm[:, p, :, :], xT[:, p, :, :], ALU.add)\
                    .then_inc(s_h, 1)

            def layer_stats(p):
                dve.wait_ge(s_h, p + 1)
                for k in range(K):
                    nc.vector.bn_stats(lst[:, p, k, :], h[:, p, k, :]).then_inc(s_bn, 1)
                for k in range(K):
                    dve.wait_ge(s_bn, 2 * K * p + k + 1)
                    nc.vector.bn_aggr(lmv[:, p, k, :], lst[:, p, k, :]).then_inc(s_bn, 1)

            def layer_eps(p):
                dve.wait_ge(s_bn, 2 * K * (p + 1))
                nc.vector.tensor_scalar(lve[:, p, :], lmv[:, p, :, 1], EPS, None, ALU.add).then_inc(s_lve, 1)

            def layer_scale(p):
                dve.wait_ge(s_lrs, p + 1)
                for k in range(BP):
                    nc.vector.tensor_scalar(u[:, p, k, :, :],
                                            h[:, p, k, :].unsqueeze(1).to_broadcast([128, 2, C]), lmv[:, p, k, 0:1],
                                            lrs[:, p, k:k + 1], ALU.subtract, ALU.mult).then_inc(s_u, 1)

            def layer_affine(p):
                if p == 0:
                    dve.wait_ge(s_zero, 8)
                dve.wait_ge(s_uTp, p + 1)
                nc.vector.tensor_scalar(uc[C:2 * C, p, :, TAPS - 2:TAPS - 2 + N],
                                        ps_uT[C:2 * C, :].rearrange("p (b n) -> p b n", b=BP),
                                        pl[C:2 * C, L_NG:L_NG + 1], pl[C:2 * C, L_NB:L_NB + 1],
                                        ALU.mult, ALU.add).then_inc(s_uchi, 1)

            def taps():
                dve.wait_ge(s_late, 16)
                dve.wait_ge(s_ident, 1)
                nc.vector.tensor_tensor(
                    conv_in[:, :, :], pl[:, L_INW:L_INW + C].unsqueeze(1).to_broadcast([128, TAPS, C]),
                    pl[:, L_CONVW:L_CONVW + TAPS].unsqueeze(2).to_broadcast([128, TAPS, C]), ALU.mult)\
                    .then_inc(s_convin, 1)
                nc.vector.tensor_scalar(diag_d[:, :], ident[:, 0:C], pl[:, L_D:L_D + 1], None, ALU.mult)\
                    .then_inc(s_diag, 1)

            def weights():
                dve.wait_ge(s_wconvp, 1)
                nc.vector.tensor_copy(conv_w[:, :, :].rearrange("p k c -> p (k c)"), ps_setup[:, 0:256])\
                    .then_inc(s_wconv, 1)
                dve.wait_ge(s_zero, 9)
                dve.wait_ge(s_half, 2)
                for b in range(BP):
                    rows = slice(C * b, C * b + C)
                    nc.vector.tensor_scalar(outw[rows, b, 0:C], pl[rows, L_OUTWT:L_OUTWT + C], half_rms[rows, :],
                                            None, ALU.mult).then_inc(s_outw, 1)
                    nc.vector.tensor_scalar(outw[rows, b, C:OC], ps_setup[rows, 256:256 + HID], half_rms[rows, :],
                                            None, ALU.mult).then_inc(s_outw, 1)

            def dt_argument(p):
                dve.wait_ge(s_dtp, p + 1)
                nc.vector.tensor_tensor(dx[:, p, :, :], ps_dt[:, 0:K * NH].rearrange("p (k h) -> p k h", k=K),
                                        pl[:, L_DTB:L_DTB + NH].unsqueeze(1).to_broadcast([128, K, NH]),
                                        ALU.add).then_inc(s_dx, 1)

            def dt_magnitude(p):
                dve.wait_ge(s_dx, p + 1)
                dxf = dx[:, p, :, :].rearrange("p k h -> p (k h)")
                nc.vector.scalar_tensor_tensor(dn[:, p, :], dxf, -1.0, dxf, ALU.mult, ALU.min)\
                    .then_inc(s_dn, 1)

            def softplus(p, step):
                e, d, r, z, w = de[:, p, :], dd[:, p, :], dr[:, p, :], dz[:, p, :], dw[:, p, :]
                q = [dq[:, p, 0, :], dq[:, p, 1, :]]
                if step == 0:
                    dve.wait_ge(s_de, p + 1)
                else:
                    dve.wait_ge(s_softplus, SOFTPLUS * p + step)
                if step == 0:
                    ins = nc.vector.tensor_scalar(d, e, 2.0, None, ALU.add)
                elif step == 1:
                    ins = nc.vector.reciprocal(r, d)
                elif step == 2:
                    ins = nc.vector.tensor_tensor(z, e, r, ALU.mult)
                elif step == 3:
                    ins = nc.vector.tensor_tensor(w, z, z, ALU.mult)
                elif step == 4:
                    ins = nc.vector.tensor_scalar(q[0], w, ART[4], None, ALU.mult)
                elif step < 8:
                    ins = nc.vector.scalar_tensor_tensor(q[step % 2 == 1], q[step % 2 == 0], ART[8 - step], w,
                                                         ALU.add, ALU.mult)
                elif step == 8:
                    ins = nc.vector.scalar_tensor_tensor(q[0], q[1], ART[0], z, ALU.add, ALU.mult)
                elif step == 9:
                    ins = nc.vector.scalar_tensor_tensor(dt[:, p, :, :].rearrange("p k h -> p (k h)"),
                                                         dx[:, p, :, :].rearrange("p k h -> p (k h)"), 0.0, q[0],
                                                         ALU.max, ALU.add)
                else:
                    if p == 0:
                        dve.wait_ge(s_nega, 1)
                    ins = nc.vector.tensor_tensor(a[:, p, :, :], dt[:, p, :, :],
                                                  neg_a[:, :].unsqueeze(1).to_broadcast([128, K, NH]), ALU.mult)
                ins.then_inc(s_softplus, 1)

            def conv_silu(p):
                dve.wait_ge(s_half_t, p + 1)
                dve.wait_ge(s_half_v, p + 1)
                nc.vector.scalar_tensor_tensor(s[:, p, :, :], half_t[:, p, :, :], 1.0, half_v[:, p, :, :],
                                               ALU.add, ALU.mult).then_inc(s_s, 1)

            def gate_silu(p):
                dve.wait_ge(s_zt, p + 1)
                nc.vector.scalar_tensor_tensor(zg[:, p, :], zt[:, p, :], 1.0, ps_z[:, N:2 * N],
                                               ALU.add, ALU.mult).then_inc(s_zg, 1)

            def own_columns(p):
                flat = dtx[:, p, :, :, :].rearrange("p k h c -> p k (h c)")
                pad = flat[:, :, 0:NH * (C + HD) - C]
                return bass.AP(pad.tensor, pad.offset, [list(pad.ap[0]), list(pad.ap[1]), [C + HD, NH], [1, HD]])

            def token_inputs(p):
                dve.wait_ge(s_sT, p + 1)
                dve.wait_ge(s_softplus, SOFTPLUS * p + 10)
                if p == 0:
                    dve.wait_ge(s_pad, 5)
                tv = ps_sT[:, :].rearrange("p (k c) -> p k c", k=K)
                nc.vector.tensor_tensor(
                    own_columns(p),
                    tv[:, :, 0:C].rearrange("p k (h d) -> p k h d", h=NH),
                    dt[:, p, :, :].unsqueeze(3).to_broadcast([128, K, NH, HD]), ALU.mult).then_inc(s_dtx, 1)
                nc.vector.tensor_copy(bT[:, p, :, :], tv[:, 0:BP, C:C + DS]).then_inc(s_bT, 1)

            def mask_products(p):
                dve.wait_ge(s_G, p + 1)
                if p == 0:
                    dve.wait_ge(s_masks, 2)
                nc.vector.tensor_tensor(gm[:, p, :, :], ps_G[:, :].rearrange("p (k t) -> p k t", k=K),
                                        upto[:, :].unsqueeze(1).to_broadcast([128, K, T]), ALU.mult)\
                    .then_inc(s_gm, 1)
                dve.wait_ge(s_gm, p + 1)

            def weigh(p, k):
                dve.wait_ge(s_decay, K * p + k + 1)
                nc.vector.tensor_tensor(att[:, p, k, :, :], decay[:, p, k, :, :],
                                        gm[:, p, k, :].unsqueeze(1).to_broadcast([128, NH, T]), ALU.mult)\
                    .then_inc(s_att, 1)

            def state_inputs(p):
                dve.wait_ge(s_decay, K * p + BP)
                dve.wait_ge(s_dtx, p + 1)
                nc.vector.tensor_tensor(
                    wdtx[:, p, :, :].rearrange("p b (h d) -> p b h d", h=NH), own_columns(p)[:, 0:BP, :, :],
                    decay[:, p, 0:BP, :, T - 1:T].to_broadcast([128, BP, NH, HD]), ALU.mult)\
                    .then_inc(s_wdtx, 1)

            def carried(p):
                dve.wait_ge(s_inter, p + 1)
                dve.wait_ge(s_carry, p + 1)
                nc.vector.tensor_tensor(yc[:, p, :], ps_mid[:, 128:128 + T], carry[:, p, :], ALU.mult)\
                    .then_inc(s_yc, 1)

            def gated(p, i):
                dve.wait_ge(s_ys, NT * p + i + 1)
                dve.wait_ge(s_zg, p + 1)
                yv = ps_ys[i][:, 0:T]
                at = slice(T * i, T * i + T)
                if i > 0:
                    dve.wait_ge(s_yc, p + 1)
                    link(nc.vector.tensor_tensor(ys[:, p, :], yv, yc[:, p, :], ALU.add))
                    yv = ys[:, p, :]
                nc.vector.tensor_tensor(y2[:, p, at], yv, zg[:, p, at], ALU.mult).then_inc(s_y2, 1)

            def mean_square(p, i):
                dve.wait_ge(s_o, NT * p + i + 1)
                nc.vector.tensor_scalar(yve[:, p, BP * i:BP * i + BP], ps_o[i][:, BP * OC:BP * OC + BP], 1.0 / C,
                                        4 * EPS, ALU.mult, ALU.add).then_inc(s_yve, 1)

            def rms_scale(p, i):
                dve.wait_ge(s_yrs, NT * p + i + 1)
                rs = yrs[:, p, BP * i:BP * i + BP].unsqueeze(2)
                ov = ps_o[i][:, 0:BP * OC].rearrange("p (b c) -> p b c", b=BP)
                nc.vector.tensor_tensor(o3[:, p, i, :].rearrange("p (b c) -> p b c", b=BP), ov[:, :, 0:C],
                                        rs.to_broadcast([128, BP, C]), ALU.mult).then_inc(s_o3, 1)
                nc.vector.tensor_tensor(q3[:, p, i, :].rearrange("p (b c) -> p b c", b=BP), ov[:, :, C:OC],
                                        rs.to_broadcast([128, BP, HID]), ALU.mult).then_inc(s_o3, 1)

            def finish(p):
                dve.wait_ge(s_outp, NT * (p + 1))
                dve.wait_ge(s_hT, p + 1)
                link(nc.vector.tensor_tensor(base[:, p, :], ps_out[:, 0:N], hT[:, p, :], ALU.add))
                dve.wait_ge(s_gatet, p + 1)
                nc.vector.scalar_tensor_tensor(res[:, p, :], ps_out[:, 0:N], gate_t[:, p:p + 1], base[:, p, :],
                                               ALU.mult, ALU.add).then_inc(s_res, 1)

            taps()
            tokens(0)
            tokens(1)
            row_max(0, 0)
            row_max(0, 1)
            row_max(1, 0)
            weights()
            row_max(1, 1)
            residual(0)
            layer_stats(0)
            layer_eps(0)
            layer_scale(0)
            residual(1)
            layer_stats(1)
            layer_eps(1)
            layer_affine(0)
            dt_argument(0)
            dt_magnitude(0)
            layer_scale(1)
            softplus(0, 0)
            softplus(0, 1)
            softplus(0, 2)
            softplus(0, 3)
            softplus(0, 4)
            softplus(0, 5)
            softplus(0, 6)
            softplus(0, 7)
            softplus(0, 8)
            softplus(0, 9)
            softplus(0, 10)
            conv_silu(0)
            gate_silu(0)
            token_inputs(0)
            layer_affine(1)
            mask_products(0)
            dt_argument(1)
            dt_magnitude(1)
            weigh(0, 0)
            weigh(0, 1)
            state_inputs(0)
            weigh(0, 2)
            weigh(0, 3)
            gated(0, 0)
            softplus(1, 0)
            softplus(1, 1)
            softplus(1, 2)
            softplus(1, 3)
            softplus(1, 4)
            softplus(1, 5)
            softplus(1, 6)
            softplus(1, 7)
            softplus(1, 8)
            softplus(1, 9)
            softplus(1, 10)
            conv_silu(1)
            carried(0)
            gated(0, 1)
            mean_square(0, 0)
            gate_silu(1)
            mean_square(0, 1)
            token_inputs(1)
            mask_products(1)
            rms_scale(0, 0)
            rms_scale(0, 1)
            weigh(1, 0)
            weigh(1, 1)
            state_inputs(1)
            weigh(1, 2)
            weigh(1, 3)
            gated(1, 0)
            finish(0)
            mean_square(1, 0)
            carried(1)
            rms_scale(1, 0)
            gated(1, 1)
            mean_square(1, 1)
            rms_scale(1, 1)
            finish(1)

        @block.tensor
        def _(pe):
            mm = nc.tensor.matmul

            def keep_busy(where, *stage):
                columns = WARM.get(stage, 0)
                while columns > 0:
                    mm(where[:, 0:min(columns, 512)], busy[:, 0:128], busy[:, 0:min(columns, 512)],
                       start=True, stop=True)
                    columns -= 512

            pe.wait_ge(s_busy, 1)
            keep_busy(ps_setup, "start", 0)
            pe.wait_ge(s_group, 2)
            pe.wait_ge(s_gsq, 1)
            gs = ps_group[:, 0:2 * PAIRS]
            mm(gs, group_mean[:, :], gmv[:, :, :].rearrange("p b m -> p (b m)"), start=True, stop=False)
            mm(gs.rearrange("p (b m) -> p b m", m=2)[:, :, 1], group_mean[:, :], gsq[:, :],
               start=False, stop=True).then_inc(s_gg, 1)
            pe.wait_ge(s_early, 16)

            mm(ps_setup[:, 0:C], pe_[0:C, E_WK:E_WK + 2 * C], pe_[0:C, E_WQ:E_WQ + C], start=True, stop=True)
            mm(ps_setup[:, C:2 * C], pe_[0:C, E_WV:E_WV + 2 * C], pe_[0:C, E_WPT:E_WPT + C],
               start=True, stop=True).then_inc(s_mixp, 1)
            pe.wait_ge(s_ident, 1)
            for p in range(PAIRS):
                pe.wait_ge(s_x[p], 16)
                for i in range(NT):
                    last = nc.tensor.transpose(ps_xT[:, (NT * p + i) * T:(NT * p + i + 1) * T],
                                               xc[:, p, T * i:T * i + T], ident[:, :])
                last.then_inc(s_xTp, 1)
            keep_busy(ps_keys, "group", 0)

            def project_keys(p):
                if p > 0:
                    pe.wait_ge(s_keys, BP * p)
                else:
                    pe.wait_ge(s_mix, BP)
                pe.wait_ge([s_xn0, s_xn1][p], 1)
                mm(ps_keys[:, 0:N], mix[:, 0, :], xn[:, p, :], start=True, stop=True).then_inc(s_keysp, 1)

            def project_values(p):
                if p > 0:
                    pe.wait_ge(s_vals, p)
                else:
                    pe.wait_ge(s_gread, 1)
                pe.wait_ge([s_xn0, s_xn1][p], 1)
                for i in range(NT):
                    last = mm(ps_vals[:, T * i:T * i + T], xn[:, p, T * i:T * i + T], mix[:, 1, :],
                              start=True, stop=True)
                last.then_inc(s_valsp, 1)

            def scores(p, b):
                if p > 0:
                    pe.wait_ge(s_prob, NT * (b + 1))
                pe.wait_ge(s_keys, BP * p + b + 1)
                for i in range(NT):
                    mm(ps_score[b][:, N * i:N * i + N], xn[:, p, T * i:T * i + T], keys[:, p, b, :],
                       start=True, stop=True).then_inc(s_score, 1)

            def transpose_prob(p, b):
                if p > 0:
                    pe.wait_ge(s_probT, BP * (p - 1) + b + 1)
                keep_busy(ps_probT[b], "transpose_prob", p, b)
                for i in range(NT):
                    pe.wait_ge(s_prob, NT * (BP * p + b) + i + 1)
                    for j in range(NT):
                        last = nc.tensor.transpose(ps_probT[b][:, N * j + T * i:N * j + T * i + T],
                                                   prob[:, p, b, i, T * j:T * j + T], ident[:, :])
                last.then_inc(s_probTp, 1)

            def attend(p, b):
                if b == 0:
                    pe.wait_ge(s_vals, PAIRS)
                    if p == 0:
                        pe.wait_ge(s_zero, 9)
                    else:
                        pe.wait_ge(s_hT, p)
                if b == 0:
                    keep_busy(ps_y, "attend", p)
                pe.wait_ge(s_probT, BP * p + b + 1)
                for i in range(NT):
                    k = BP * i + b
                    for j in range(NT):
                        last = mm(ps_y[:, (C + 1) * k:(C + 1) * (k + 1)], probT[:, p, b, j, T * i:T * i + T],
                                  vals[:, p, BP * j + b, :], start=(j == 0), stop=(j == NT - 1))
                if b == BP - 1:
                    last.then_inc(s_y, 1)

            def transpose_h(p):
                pe.wait_ge(s_yread, p + 1)
                keep_busy(ps_y, "transpose_h", p)
                pe.wait_ge(s_h, p + 1)
                for i in range(NT):
                    last = nc.tensor.transpose(ps_y[:, T * i:T * i + T],
                                               h[:, p, BP * i:BP * i + BP, :].rearrange("p b c -> p (b c)"),
                                               ident[:, :])
                last.then_inc(s_hTp, 1)

            def weights():
                pe.wait_ge(s_convin, 1)
                pe.wait_ge(s_mix, BP)
                for j in range(2):
                    nc.tensor.transpose(ps_setup[:, T * j:T * j + T],
                                        conv_in[:, 2 * j:2 * j + 2, :].rearrange("p k c -> p (k c)"),
                                        ident[:, :])
                mm(ps_setup[:, 256:256 + HID], pl[0:C, L_OUTW:L_OUTW + 2 * C], pl[0:C, L_SE1T:L_SE1T + HID],
                   start=True, stop=True).then_inc(s_wconvp, 1)

            def transpose_u(p):
                if p == 0:
                    pe.wait_ge(s_xT, PAIRS)
                else:
                    pe.wait_ge(s_bT, p)
                keep_busy(ps_uT, "transpose_u", p)
                for k in range(K):
                    i, b = divmod(k, BP)
                    if k < BP:
                        pe.wait_ge(s_u, BP * p + k + 1)
                    else:
                        pe.wait_ge(s_upool, BP * p + k - BP + 1)
                    last = nc.tensor.transpose(ps_uT[:, N * b + T * i:N * b + T * i + T],
                                               u[:, p, k, :, :].rearrange("p j c -> p (j c)"),
                                               ident[:, :])
                last.then_inc(s_uTp, 1)

            def project_dt(p):
                if p == 0:
                    pe.wait_ge(s_keys, BP * PAIRS)
                else:
                    pe.wait_ge(s_zg, p)
                keep_busy(ps_dt, "project_dt", p)
                pe.wait_ge(s_uclo, p + 1)
                pe.wait_ge(s_uchi, p + 1)
                for k in range(K):
                    i, b = divmod(k, BP)
                    at = TAPS - 1 + T * i
                    last = mm(ps_dt[:, NH * k:NH * k + NH], uc[:, p, b, at:at + T],
                              pl[:, L_WDT:L_WDT + NH], start=True, stop=True)
                last.then_inc(s_dtp, 1)

            def project_z(p):
                pe.wait_ge(s_dx, p + 1)
                for b in range(BP):
                    last = mm(ps_z[C * b:C * b + C, N:2 * N], pl[:, L_WZ:L_WZ + C],
                              uc[:, p, b, TAPS - 1:TAPS - 1 + N], start=True, stop=True)
                last.then_inc(s_zp, 1)

            def convolve(p):
                pe.wait_ge(s_uclo, p + 1)
                pe.wait_ge(s_uchi, p + 1)
                if p == 0:
                    pe.wait_ge(s_wconv, 1)
                    pe.wait_ge(s_outw, 2 * BP)
                else:
                    pe.wait_ge(s_gm, p)
                for j in range(2):
                    last = mm(ps_conv[:, :], conv_w[:, j, :], uc[:, p, :, 2 * j:2 * j + N],
                              start=(j == 0), stop=(j == 1))
                last.then_inc(s_conv, 1)

            def transpose_s(p):
                pe.wait_ge(s_uclo, p + 1)
                pe.wait_ge(s_uchi, p + 1)
                if p > 0:
                    pe.wait_ge(s_yc, p)
                keep_busy(ps_sT, "transpose_s", p)
                pe.wait_ge(s_s, p + 1)
                for k in range(K):
                    i, b = divmod(k, BP)
                    last = nc.tensor.transpose(ps_sT[:, T * k:T * k + T], s[:, p, b, T * i:T * i + T], ident[:, :])
                last.then_inc(s_sT, 1)

            def products(p):
                pe.wait_ge(s_cs, p + 1)
                for k in range(K):
                    i, b = divmod(k, BP)
                    last = mm(ps_G[:, T * k:T * k + T], s[:, p, b, T * i:T * i + T],
                              cs[:, p, b, T * i:T * i + T], start=True, stop=True)
                last.then_inc(s_G, 1)

            def segment_sums(p, k):
                if p == 0 and k == 0:
                    pe.wait_ge(s_masks, 1)
                    pe.wait_ge(s_prob, NT * B)
                    pe.wait_ge(s_probT, B)
                before = K * p + k - len(ps_S)
                if before >= 0:
                    pe.wait_ge(s_decay, before + 1)
                keep_busy(ps_S[(K * p + k) % len(ps_S)], "segment_sums", p, k)
                pe.wait_ge(s_am, K * p + k + 1)
                mm(ps_S[(K * p + k) % len(ps_S)][:, :], after[:, :], am[:, p, k, :, :].rearrange("p h t -> p (h t)"),
                   start=True, stop=True).then_inc(s_S, 1)

            def chunk_state(p):
                pe.wait_ge(s_bT, p + 1)
                keep_busy(ps_mid, "chunk_state", p)
                pe.wait_ge(s_wdtx, p + 1)
                for b in range(BP):
                    mm(ps_mid[C:C + DS, C * b:C * b + C], bT[:, p, b, :], wdtx[:, p, b, :],
                       start=True, stop=True)
                if p == 0:
                    pe.wait_ge(s_masks, 2)
                pe.wait_ge(s_awide, p + 1)
                mm(ps_mid[:, 256:256 + T], a_wide[:, p, :, :, :].rearrange("p b h d -> p (b h d)"), upto[:, :],
                   start=True, stop=True).then_inc(s_statep, 1)

            def carried(p):
                pe.wait_ge(s_state, p + 1)
                pe.wait_ge(s_carry, p + 1)
                for b in range(BP):
                    last = mm(ps_mid[C * b:C * b + C, 128:128 + T], state[:, p, b, :], cs[:, p, b, T:2 * T],
                              start=True, stop=True)
                last.then_inc(s_inter, 1)

            def chunk_output(p, k):
                i, b = divmod(k, BP)
                if k == 0:
                    if p == 0:
                        pe.wait_ge(s_diag, 1)
                        pe.wait_ge(s_hT, PAIRS)
                    pe.wait_ge(s_dtx, p + 1)
                if p > 0 and b == 0:
                    pe.wait_ge(s_o3, 2 * (NT * (p - 1) + i + 1))
                if b == 0:
                    keep_busy(ps_ys[i], "chunk_output", p, i)
                rows = ps_ys[i][C * b:C * b + C, 0:T]
                mm(rows, diag_d[:, :], s[:, p, b, T * i:T * i + T], start=True, stop=False)
                pe.wait_ge(s_att, K * p + k + 1)
                for hd in range(NH):
                    last = mm(rows, dtx[:, p, k, hd, :], att[:, p, k, hd, :], start=False, stop=(hd == NH - 1))
                if b == BP - 1:
                    last.then_inc(s_ys, 1)

            def out_project(p, i):
                keep_busy(ps_o[i], "out_project", p, i)
                pe.wait_ge(s_y2, NT * p + i + 1)
                mm(ps_o[i][:, 0:BP * OC], y2[:, p, T * i:T * i + T], outw[:, :, :].rearrange("p b c -> p (b c)"),
                   start=True, stop=True)
                pe.wait_ge(s_ysq, NT * p + i + 1)
                mm(ps_o[i][:, BP * OC:BP * OC + BP], ysq[:, p, T * i:T * i + T], pl[:, L_PICK:L_PICK + BP],
                   start=True, stop=True).then_inc(s_o, 1)

            def transpose_out(p, i):
                if i == 0:
                    pe.wait_ge(s_gm, min(p + 2, PAIRS))
                    if p > 0:
                        pe.wait_ge(s_res, p)
                keep_busy(ps_out[:, :], "transpose_out", p, i)
                pe.wait_ge(s_o3, 2 * (NT * p + i) + 1)
                nc.tensor.transpose(ps_out[:, T * i:T * i + T], o3[:, p, i, :], ident[:, :]).then_inc(s_outp, 1)

            def squeeze(p):
                if p == 0:
                    pe.wait_ge(s_zg, PAIRS)
                else:
                    pe.wait_ge(s_gatet, p)
                pe.wait_ge(s_o3, 2 * NT * (p + 1))
                for i in range(NT):
                    last = mm(ps_se[0:BP * HID, 0:1], q3[:, p, i, :], ones[:, :], start=(i == 0),
                              stop=(i == NT - 1))
                last.then_inc(s_hidp, 1)
                pe.wait_ge(s_hid, p + 1)
                mm(ps_se[:, 1:2], pl[0:BP * HID, L_SE2T:L_SE2T + 128], hidden[:, p:p + 1],
                   start=True, stop=True).then_inc(s_gatep, 1)

            project_keys(0)
            project_keys(1)
            scores(0, 0)
            project_values(0)
            scores(0, 1)
            project_values(1)
            weights()
            scores(1, 0)
            transpose_prob(0, 0)
            transpose_prob(0, 1)
            scores(1, 1)
            attend(0, 0)
            attend(0, 1)
            transpose_prob(1, 0)
            transpose_prob(1, 1)
            transpose_h(0)
            attend(1, 0)
            attend(1, 1)
            transpose_u(0)
            project_dt(0)
            convolve(0)
            project_z(0)
            transpose_h(1)
            transpose_s(0)
            products(0)
            transpose_u(1)
            project_dt(1)
            segment_sums(0, 0)
            segment_sums(0, 1)
            segment_sums(0, 2)
            segment_sums(0, 3)
            chunk_output(0, 0)
            chunk_output(0, 1)
            convolve(1)
            project_z(1)
            chunk_state(0)
            carried(0)
            chunk_output(0, 2)
            chunk_output(0, 3)
            out_project(0, 0)
            transpose_s(1)
            products(1)
            out_project(0, 1)
            segment_sums(1, 0)
            segment_sums(1, 1)
            segment_sums(1, 2)
            segment_sums(1, 3)
            transpose_out(0, 0)
            transpose_out(0, 1)
            chunk_output(1, 0)
            chunk_output(1, 1)
            squeeze(0)
            chunk_state(1)
            carried(1)
            out_project(1, 0)
            chunk_output(1, 2)
            chunk_output(1, 3)
            transpose_out(1, 0)
            out_project(1, 1)
            transpose_out(1, 1)
            squeeze(1)


def kernel(**inputs):
    import numpy as np
    import concourse.bacc as bacc
    from concourse.bass_utils import run_bass_kernel_spmd

    f = {name: np.asarray(value) for name, value in inputs.items()}

    def column(v, rows=128):
        col = np.zeros((128, 1), np.float32)
        col[:rows, 0] = np.concatenate([v] * (rows // v.shape[0]))
        return col

    def row(v):
        return np.ascontiguousarray(np.broadcast_to(v[None, :], (128, v.shape[0])))

    def top(m):
        full = np.zeros((128, m.shape[1]), np.float32)
        full[:m.shape[0]] = m
        return full

    def twice(m):
        return np.concatenate([m, m], axis=1)

    def diagonal(m):
        r, c = m.shape
        full = np.zeros((128, BP * c), np.float32)
        for b in range(BP):
            full[r * b:r * b + r, c * b:c * b + c] = m
        return full

    w = f["L0_conv_w_qkv"]
    early = np.concatenate([
        column(f["L0_conv_gamma"]), column(f["L0_conv_beta"]),
        top(w[0:C]), top(twice(w[C:2 * C])), top(twice(w[2 * C:3 * C])), top(f["L0_conv_w_proj"].T),
        row(f["L0_conv_b_proj"])], axis=1)
    inw = f["L1_conv_in_w"]
    xbc = inw[C:C + 128]
    wz, wdt = inw[0:C], inw[C + 128:]
    late = np.concatenate([
        column(f["L1_conv_norm_g"]), column(f["L1_conv_norm_b"]), column(f["L1_conv_rms_w"]),
        column(np.repeat(f["L1_conv_Dp"], HD)), column(f["L1_conv_conv_b"]), column(f["L1_conv_se2_b"]),
        column(f["L1_conv_se1_b"], BP * HID), np.zeros((128, 1), np.float32),
        f["L1_conv_conv_w"], row(f["L1_conv_dt_bias"]), row(f["L1_conv_A_log"]),
        xbc, top(wz.T), top(wdt.T), top(twice(f["L1_conv_out_w"])), np.concatenate([f["L1_conv_out_w"].T] * BP),
        top(f["L1_conv_se1_w"].T), diagonal(f["L1_conv_se2_w"].T), diagonal(np.ones((C, 1), np.float32))], axis=1)

    fp32 = mybir.dt.float32
    nc = bacc.Bacc("TRN2", target_bir_lowering=False, num_devices=1)
    arrays = {"in_x": np.ascontiguousarray(f["x"]), "in_early": early, "in_late": late}
    args = [nc.dram_tensor(n, v.shape, fp32, kind="ExternalInput").ap() for n, v in arrays.items()]
    args.append(nc.dram_tensor("out_0", f["x"].shape, fp32, kind="ExternalOutput").ap())
    attention_mamba_kernel(nc, *args)
    r = run_bass_kernel_spmd(nc, [arrays], core_ids=[0])
    return r.results[0]["out_0"]
```

```python
import concourse.bass as bass
from concourse import mybir
from contextlib import ExitStack
import math

B, C, N = 4, 64, 256
BP = 2
PAIRS = B // BP
T = 128
NT = N // T
K = NT * BP
GROUP = C // 8
NH, HD, DS = 4, 16, 32
TAPS = 4
HID = C // 4
OC = C + HID
UP = N + TAPS
EPS = 1e-5
SOFTPLUS = 11
WARM = {
    ("start", 0): 3584,
    ("project_dt", 0): 1024,
    ("transpose_s", 0): 1024,
    ("attend", 1): 512,
    ("chunk_state", 1): 512,
    ("segment_sums", 1, 2): 512,
    ("segment_sums", 1, 3): 512,
}

E_GAMMA, E_BETA, E_WQ, E_WK, E_WV, E_WPT, E_BPROJ = 0, 1, 2, 66, 194, 322, 386
E_COLS = 450
L_NG, L_NB, L_RMS, L_D, L_CONVB, L_SE2B, L_SE1B = 0, 1, 2, 3, 4, 5, 6
L_CONVW, L_DTB, L_ALOG, L_INW, L_WZ, L_WDT = 8, 12, 16, 20, 84, 148
L_OUTW, L_OUTWT, L_SE1T, L_SE2T = 152, 280, 344, 360
L_PICK = 488
L_COLS = 490


def artanh_coefficients(degree):
    import numpy as np
    k = np.arange(64)
    w = (1 + np.cos(np.pi * (k + 0.5) / 64)) / 18
    z = np.sqrt(w)
    fit = np.polynomial.chebyshev.Chebyshev.fit(w, 2 * np.arctanh(z) / z, degree, domain=[0, 1 / 9])
    return [float(c) for c in fit.convert(kind=np.polynomial.Polynomial).coef]


def attention_mamba_kernel(nc: bass.Bass, x: bass.AP, early: bass.AP, late: bass.AP, out: bass.AP):
    fp32 = mybir.dt.float32
    ALU = mybir.AluOpType
    ACT = mybir.ActivationFunctionType
    AX = mybir.AxisListType
    ART = artanh_coefficients(4)

    x_v = x.rearrange("(p b) c h w -> p (b c) (h w)", b=BP)
    out_v = out.rearrange("(p b) c h w -> p (b c) (h w)", b=BP)

    ctx = ExitStack()
    with ctx:
        def sb(name, shape):
            return ctx.enter_context(nc.sbuf_tensor(name, shape, fp32))

        busy = ctx.enter_context(nc.sbuf_tensor("busy", [128, 512], mybir.dt.bfloat16))

        def sem(name):
            return ctx.enter_context(nc.semaphore(name))

        xc = sb("xc", [128, PAIRS, N])
        pe_ = sb("params_early", [128, E_COLS])
        pl = sb("params_late", [128, L_COLS])
        ident = sb("ident", [128, 128])
        group_mean = sb("group_mean", [128, 128])
        after = sb("after", [128, 128])
        upto = sb("upto", [128, 128])
        minus_half = sb("minus_half", [128, 4])

        mix = sb("mix", [128, 2, 128])
        conv_in = sb("conv_in", [128, TAPS, C])
        conv_w = sb("conv_w", [128, 2, 128])
        diag_d = sb("diag_d", [128, C])
        outw = sb("outw", [128, BP, OC])
        ones = sb("ones", [128, 1])
        neg_a = sb("neg_a", [128, NH])
        half_bias = sb("half_bias", [128, 2])
        rms_gain = sb("rms_gain", [128, 1])

        gst = sb("gst", [128, PAIRS, 6])
        gmv = sb("gmv", [128, PAIRS, 3])
        gg = sb("gg", [128, PAIRS, 3])
        ggsq = sb("ggsq", [128, PAIRS])
        gms = sb("gms", [128, PAIRS])
        gve = sb("gve", [128, PAIRS])
        grs = sb("grs", [128, PAIRS])
        gscale = sb("gscale", [128, PAIRS])
        xm = sb("xm", [128, PAIRS, N])
        xn = sb("xn", [128, PAIRS, N])

        keys = sb("keys", [128, PAIRS, BP, N])
        vals = sb("vals", [128, PAIRS, K, C + 1])
        xT = sb("xT", [128, PAIRS, K, C])
        neg_max = sb("neg_max", [128, PAIRS, BP, NT])
        prob = sb("prob", [128, PAIRS, BP, NT, N])
        probT = sb("probT", [128, PAIRS, BP, NT, N])
        rden = sb("rden", [128, PAIRS, BP, NT])
        h = sb("h", [128, PAIRS, K, C])
        hT = sb("hT", [128, PAIRS, N])

        lst = sb("lst", [128, PAIRS, K, 6])
        lmv = sb("lmv", [128, PAIRS, K, 2])
        lve = sb("lve", [128, PAIRS, BP, NT])
        lrs = sb("lrs", [128, PAIRS, BP, NT])
        u = sb("u", [128, PAIRS, K, 2, C])
        uc = sb("uc", [128, PAIRS, BP, UP])
        half_v = sb("half_v", [128, PAIRS, BP, N])
        half_t = sb("half_t", [128, PAIRS, BP, N])
        s = sb("s", [128, PAIRS, BP, N])
        cs = sb("cs", [128, PAIRS, BP, N])
        zt = sb("zt", [128, PAIRS, N])
        zg = sb("zg", [128, PAIRS, N])

        dx = sb("dx", [128, PAIRS, K, NH])
        dn = sb("dn", [128, PAIRS, K * NH])
        de = sb("de", [128, PAIRS, K * NH])
        dd = sb("dd", [128, PAIRS, K * NH])
        dr = sb("dr", [128, PAIRS, K * NH])
        dz = sb("dz", [128, PAIRS, K * NH])
        dw = sb("dw", [128, PAIRS, K * NH])
        dq = sb("dq", [128, PAIRS, 2, K * NH])
        dt = sb("dt", [128, PAIRS, K, NH])
        a = sb("a", [128, PAIRS, K, NH])

        am = sb("am", [128, PAIRS, K, NH, T])
        decay = sb("decay", [128, PAIRS, K, NH, T])
        gm = sb("gm", [128, PAIRS, K, T])
        att = sb("att", [128, PAIRS, K, NH, T])
        dtx = sb("dtx", [128, PAIRS, K, NH, C])
        bT = sb("bT", [128, PAIRS, BP, DS])
        wdtx = sb("wdtx", [128, PAIRS, BP, C])
        state = sb("state", [128, PAIRS, BP, C])
        a_wide = sb("a_wide", [128, PAIRS, BP, NH, HD])
        carry = sb("carry", [128, PAIRS, T])
        yc = sb("yc", [128, PAIRS, T])

        y2 = sb("y2", [128, PAIRS, N])
        ysq = sb("ysq", [128, PAIRS, N])
        yve = sb("yve", [128, PAIRS, K])
        yrs = sb("yrs", [128, PAIRS, K])
        o3 = sb("o3", [128, PAIRS, NT, BP * C])
        q3 = sb("q3", [128, PAIRS, NT, BP * HID])
        hidden = sb("hidden", [BP * HID, PAIRS])
        gate_t = sb("gate_t", [128, PAIRS])
        base = sb("base", [128, PAIRS, N])
        res = sb("res", [128, PAIRS, N])

        bank = [ctx.enter_context(nc.psum_tensor(f"bank{i}", [128, 512], fp32)) for i in range(8)]
        ps_setup = bank[7]
        ps_group = bank[5]
        ps_xT = bank[6]
        ps_keys = [bank[0], bank[3]]
        ps_vals = [bank[5], bank[4]]
        ps_score = [bank[1], bank[2]]
        ps_probT = [bank[3], bank[4]]
        ps_y = [bank[5], bank[7]]
        ps_hT = bank[5]
        ps_uT = bank[6]
        ps_conv = bank[7]
        ps_dt = bank[0]
        ps_z = bank[0]
        ps_sT = bank[6]
        ps_G = bank[7]
        ps_S = [bank[1], bank[2], bank[3]]
        ps_ys = [bank[5], bank[4]]
        ps_mid = bank[6]
        ps_o = [bank[5], bank[4]]
        ps_out = bank[7]
        ps_se = bank[0]

        s_x = [sem(f"s_x{p}") for p in range(PAIRS)]
        s_early, s_late, s_out = sem("s_early"), sem("s_late"), sem("s_out")
        s_zero, s_ident, s_group, s_masks = sem("s_zero"), sem("s_ident"), sem("s_group"), sem("s_masks")
        s_mixp, s_mix = sem("s_mixp"), sem("s_mix")
        s_gsq, s_gg, s_gve, s_grs = sem("s_gsq"), sem("s_gg"), sem("s_gve"), sem("s_grs")
        s_gread, s_gscale, s_xm, s_xn0, s_xn1 = (sem("s_gread"), sem("s_gscale"), sem("s_xm"), sem("s_xn0"),
                                                 sem("s_xn1"))
        s_busy, s_pad = sem("s_busy"), sem("s_pad")
        s_xTp, s_xT = sem("s_xTp"), sem("s_xT")
        s_keysp, s_valsp, s_vals = sem("s_keysp"), sem("s_valsp"), sem("s_vals")
        s_keys = [sem(f"s_keys{b}") for b in range(BP)]
        s_score, s_max, s_prob, s_probTp = sem("s_score"), sem("s_max"), sem("s_prob"), sem("s_probTp")
        s_probT = sem("s_probT")
        s_y, s_h, s_hTp, s_hT = sem("s_y"), sem("s_h"), sem("s_hTp"), sem("s_hT")
        s_lve, s_lrs, s_u, s_uTp = sem("s_lve"), sem("s_lrs"), sem("s_u"), sem("s_uTp")
        s_uclo, s_uchi = sem("s_uclo"), sem("s_uchi")
        s_convin, s_wconvp, s_wconv, s_outw = sem("s_convin"), sem("s_wconvp"), sem("s_wconv"), sem("s_outw")
        s_nega, s_diag, s_half = sem("s_nega"), sem("s_diag"), sem("s_half")
        s_conv, s_half_v, s_half_t, s_s, s_cs = (sem("s_conv"), sem("s_half_v"), sem("s_half_t"),
                                                 sem("s_s"), sem("s_cs"))
        s_dtp, s_zp, s_zt, s_zg, s_dx = sem("s_dtp"), sem("s_zp"), sem("s_zt"), sem("s_zg"), sem("s_dx")
        s_dn, s_de, s_softplus = sem("s_dn"), sem("s_de"), sem("s_softplus")
        s_am, s_S, s_decay = sem("s_am"), sem("s_S"), sem("s_decay")
        s_sT, s_dtx, s_bT, s_G, s_gm, s_att = (sem("s_sT"), sem("s_dtx"), sem("s_bT"), sem("s_G"),
                                               sem("s_gm"), sem("s_att"))
        s_wdtx, s_statep, s_state, s_awide, s_carry = (sem("s_wdtx"), sem("s_statep"), sem("s_state"),
                                                       sem("s_awide"), sem("s_carry"))
        s_inter, s_ys, s_yc, s_y2, s_ysq = sem("s_inter"), sem("s_ys"), sem("s_yc"), sem("s_y2"), sem("s_ysq")
        s_o, s_yve, s_yrs = sem("s_o"), sem("s_yve"), sem("s_yrs")
        s_q3, s_o3, s_outp = sem("s_q3"), sem("s_o3"), sem("s_outp")
        s_hidp, s_hid, s_gatep, s_gatet = sem("s_hidp"), sem("s_hid"), sem("s_gatep"), sem("s_gatet")
        s_res = sem("s_res")
        s_vec, s_act = sem("s_vec"), sem("s_act")
        s_bn = sem("s_bn")

        block = ctx.enter_context(nc.Block())

        @block.sync
        def _(sync):
            sync.dma_start(xc[:, 0, :], x_v[0]).then_inc(s_x[0], 16)
            sync.dma_start(pe_[:, :], early).then_inc(s_early, 16)
            for p in range(PAIRS):
                sync.wait_ge(s_res, p + 1)
                sync.dma_start(out_v[p], res[:, p, :]).then_inc(s_out, 16)
            sync.wait_ge(s_out, 16 * PAIRS)

        @block.gpsimd
        def _(pool):
            nc.gpsimd.memset(busy[:, :], 0.0).then_inc(s_busy, 1)
            nc.gpsimd.memset(group_mean[:, :], 1.0 / GROUP).then_inc(s_zero, 1)
            nc.gpsimd.memset(ident[:, :], 0.0).then_inc(s_zero, 1)
            nc.gpsimd.memset(minus_half[:, :], -0.5).then_inc(s_zero, 1)
            nc.gpsimd.memset(mix[:, :, :], 0.0).then_inc(s_zero, 1)
            pool.wait_ge(s_zero, 4)
            gv = group_mean[:, :].rearrange("c (g j) -> c g j", j=GROUP)
            gpat = [[-GROUP, 128 // GROUP], [0, GROUP]]
            nc.gpsimd.affine_select(out=gv, in_=gv, compare_op=ALU.is_ge, fill=0.0, base=0, pattern=gpat,
                                    channel_multiplier=1).then_inc(s_group, 1)
            pool.wait_ge(s_group, 1)
            nc.gpsimd.affine_select(out=gv, in_=gv, compare_op=ALU.is_ge, fill=0.0, base=GROUP - 1,
                                    pattern=[[GROUP, 128 // GROUP], [0, GROUP]],
                                    channel_multiplier=-1).then_inc(s_group, 1)
            nc.gpsimd.affine_select(out=ident[:, :], in_=ident[:, :], compare_op=ALU.not_equal, fill=1.0,
                                    base=0, pattern=[[-1, 128]], channel_multiplier=1).then_inc(s_ident, 1)
            nc.gpsimd.memset(keys[:, :, :, :], 0.0).then_inc(s_pad, 1)
            nc.gpsimd.memset(after[:, :], 1.0).then_inc(s_zero, 1)
            nc.gpsimd.memset(upto[:, :], 1.0).then_inc(s_zero, 1)
            nc.gpsimd.memset(outw[:, :, :], 0.0).then_inc(s_zero, 1)
            nc.gpsimd.memset(uc[:, :, :, :], 0.0).then_inc(s_zero, 1)
            nc.gpsimd.memset(vals[:, :, :, C:C + 1], 1.0).then_inc(s_zero, 1)
            pool.wait_ge(s_zero, 9)
            nc.gpsimd.affine_select(out=after[:, :], in_=after[:, :], compare_op=ALU.is_gt, fill=0.0, base=0,
                                    pattern=[[-1, 128]], channel_multiplier=1).then_inc(s_masks, 1)
            nc.gpsimd.affine_select(out=upto[:, :], in_=upto[:, :], compare_op=ALU.is_ge, fill=0.0, base=0,
                                    pattern=[[1, 128]], channel_multiplier=-1).then_inc(s_masks, 1)
            pool.wait_ge(s_gve, 1)
            pool.wait_ge(s_early, 16)
            nc.gpsimd.tensor_tensor(grs[:, :], gve[:, :], minus_half[:, 0:PAIRS], ALU.pow).then_inc(s_grs, 1)
            pool.wait_ge(s_grs, 1)
            nc.gpsimd.tensor_tensor(gscale[:, :], grs[:, :], pe_[:, E_GAMMA:E_GAMMA + 1].to_broadcast([128, PAIRS]),
                                    ALU.mult).then_inc(s_gscale, 1)

            nc.gpsimd.memset(cs[:, :, :, :], 0.0).then_inc(s_pad, 1)
            nc.gpsimd.memset(state[:, :, :, :], 0.0).then_inc(s_pad, 1)
            nc.gpsimd.memset(ones[:, :], 1.0).then_inc(s_pad, 1)
            nc.gpsimd.memset(dtx[:, :, :, :, :], 0.0).then_inc(s_pad, 1)

            def layer_rstd(p, b):
                pool.wait_ge(s_lve, BP * p + b + 1)
                nc.gpsimd.tensor_tensor(lrs[:, p, b, :], lve[:, p, b, :], minus_half[:, 0:NT], ALU.pow)\
                    .then_inc(s_lrs, 1)

            def masked_decay(p, k):
                pool.wait_ge(s_softplus, SOFTPLUS * (p + 1))
                nc.gpsimd.affine_select(
                    out=am[:, p, k, :, :], in_=a[:, p, k, :].unsqueeze(2).to_broadcast([128, NH, T]),
                    compare_op=ALU.is_ge, fill=0.0, base=0, pattern=[[0, NH], [1, T]],
                    channel_multiplier=-1).then_inc(s_am, 1)

            def wide_decay(p):
                pool.wait_ge(s_softplus, SOFTPLUS * (p + 1))
                nc.gpsimd.tensor_copy(a_wide[:, p, :, :, :],
                                      a[:, p, BP:K, :].unsqueeze(3).to_broadcast([128, BP, NH, HD]))\
                    .then_inc(s_awide, 1)

            def rms_rstd(p, i):
                pool.wait_ge(s_yve, NT * p + i + 1)
                nc.gpsimd.tensor_tensor(yrs[:, p, BP * i:BP * i + BP], yve[:, p, BP * i:BP * i + BP],
                                        minus_half[:, 0:BP], ALU.pow).then_inc(s_yrs, 1)

            layer_rstd(0, 0)
            layer_rstd(0, 1)
            layer_rstd(1, 0)
            layer_rstd(1, 1)
            masked_decay(0, 0)
            masked_decay(0, 1)
            masked_decay(0, 2)
            masked_decay(0, 3)
            wide_decay(0)
            masked_decay(1, 0)
            masked_decay(1, 1)
            masked_decay(1, 2)
            masked_decay(1, 3)
            rms_rstd(0, 0)
            wide_decay(1)
            rms_rstd(0, 1)
            rms_rstd(1, 0)
            rms_rstd(1, 1)

        @block.scalar
        def _(act):
            done = [0]

            def link(ins):
                done[0] += 1
                ins.then_inc(s_act, 1)
                act.wait_ge(s_act, done[0])

            act.dma_start(xc[:, 1, :], x_v[1]).then_inc(s_x[1], 16)
            act.dma_start(pl[:, :], late).then_inc(s_late, 16)

            act.wait_ge(s_mixp, 1)
            act.wait_ge(s_zero, 4)
            mp = ps_setup[:, 0:2 * C].rearrange("p (m c) -> p m c", m=2)
            for b in range(BP):
                nc.scalar.activation(mix[C * b:C * b + C, :, C * b:C * b + C], mp[C * b:C * b + C, :, :],
                                     ACT.Copy).then_inc(s_mix, 1)
            act.wait_ge(s_late, 16)
            link(nc.scalar.activation(neg_a[:, :], pl[:, L_ALOG:L_ALOG + NH], ACT.Exp))
            nc.scalar.mul(neg_a[:, :], neg_a[:, :], -1.0).then_inc(s_nega, 1)
            nc.scalar.mul(half_bias[:, :], pl[:, L_CONVB:L_CONVB + 2], 0.5).then_inc(s_half, 1)
            nc.scalar.mul(rms_gain[:, :], pl[:, L_RMS:L_RMS + 1], 0.5 * C ** 0.5).then_inc(s_half, 1)

            def group_norm(p):
                act.wait_ge(s_gscale, 1)
                act.wait_ge(s_xm, 1)
                nc.scalar.activation(xn[:, p, :], xm[:, p, :], ACT.Identity, scale=gscale[:, p:p + 1],
                                     bias=pe_[:, E_BETA:E_BETA + 1]).then_inc(s_xn1, 1)

            def keys_copy(p):
                act.wait_ge(s_keysp, p + 1)
                if p == 0:
                    act.wait_ge(s_pad, 1)
                nc.scalar.activation(keys[0:C, p, 0, :], ps_keys[p][0:C, 0:N], ACT.Copy, scale=C ** -0.5)\
                    .then_inc(s_keys[0], 1)

            def values_copy(p):
                act.wait_ge(s_valsp, p + 1)
                nc.scalar.activation(vals[:, p, :, 0:C],
                                     ps_vals[p][:, 0:N].rearrange("p (k c) -> p k c", k=K), ACT.Copy)\
                    .then_inc(s_vals, 1)

            def softmax(p, b):
                act.wait_ge(s_max, BP * p + b + 1)
                for i in range(NT):
                    nc.scalar.activation(prob[:, p, b, i, :], ps_score[b][:, N * i:N * i + N], ACT.Exp,
                                         bias=neg_max[:, p, b, i:i + 1]).then_inc(s_prob, 1)

            def probT_copy(p, b):
                act.wait_ge(s_probTp, BP * p + b + 1)
                nc.scalar.activation(probT[:, p, b, :, :].rearrange("p i n -> p (i n)"), ps_probT[b][:, :],
                                     ACT.Copy).then_inc(s_probT, 1)

            def h_copy(p):
                act.wait_ge(s_hTp, p + 1)
                nc.scalar.activation(hT[:, p, :], ps_hT[:, 0:N], ACT.Copy).then_inc(s_hT, 1)

            def layer_affine(p):
                if p == 0:
                    act.wait_ge(s_zero, 8)
                act.wait_ge(s_uTp, p + 1)
                nc.scalar.activation(uc[0:C, p, :, TAPS - 1:TAPS - 1 + N],
                                     ps_uT[0:C, :].rearrange("p (b n) -> p b n", b=BP), ACT.Identity,
                                     scale=pl[0:C, L_NG:L_NG + 1], bias=pl[0:C, L_NB:L_NB + 1])\
                    .then_inc(s_uclo, 1)

            def layer_affine_delayed(p):
                act.wait_ge(s_uTp, p + 1)
                nc.scalar.activation(uc[C:2 * C, p, :, TAPS - 2:TAPS - 2 + N],
                                     ps_uT[C:2 * C, :].rearrange("p (b n) -> p b n", b=BP), ACT.Identity,
                                     scale=pl[C:2 * C, L_NG:L_NG + 1], bias=pl[C:2 * C, L_NB:L_NB + 1])\
                    .then_inc(s_uchi, 1)

            def gate_tanh(p):
                act.wait_ge(s_zp, p + 1)
                nc.scalar.activation(zt[:, p, :], ps_z[:, N:2 * N], ACT.Tanh, scale=0.5).then_inc(s_zt, 1)

            def conv_silu(p):
                if p == 0:
                    act.wait_ge(s_half, 2)
                act.wait_ge(s_conv, p + 1)
                cv = ps_conv[:, :]
                nc.scalar.activation(half_t[:, p, :, :].rearrange("p b n -> p (b n)"), cv, ACT.Tanh,
                                     scale=0.5, bias=half_bias[:, 0:1]).then_inc(s_half_t, 1)
                nc.scalar.activation(half_v[:, p, :, :].rearrange("p b n -> p (b n)"), cv, ACT.Identity,
                                     scale=0.5, bias=half_bias[:, 0:1]).then_inc(s_half_v, 1)

            def c_copy(p):
                if p == 0:
                    act.wait_ge(s_pad, 3)
                act.wait_ge(s_s, p + 1)
                nc.scalar.activation(cs[C:C + DS, p, :, :], s[C + DS:C + 2 * DS, p, :, :], ACT.Copy)\
                    .then_inc(s_cs, 1)

            def dt_exp(p):
                act.wait_ge(s_dn, p + 1)
                nc.scalar.activation(de[:, p, :], dn[:, p, :], ACT.Exp).then_inc(s_de, 1)

            def decays(p, k):
                act.wait_ge(s_S, K * p + k + 1)
                nc.scalar.activation(decay[:, p, k, :, :].rearrange("p h t -> p (h t)"),
                                     ps_S[(K * p + k) % len(ps_S)][:, :],
                                     ACT.Exp).then_inc(s_decay, 1)

            def chunk_state(p):
                if p == 0:
                    act.wait_ge(s_pad, 3)
                act.wait_ge(s_statep, p + 1)
                nc.scalar.activation(state[C:C + DS, p, :, :].rearrange("p b c -> p (b c)"),
                                     ps_mid[C:C + DS, 0:BP * C], ACT.Copy).then_inc(s_state, 1)
                nc.scalar.activation(carry[:, p, :], ps_mid[:, 256:256 + T], ACT.Exp).then_inc(s_carry, 1)

            def square(p, i):
                act.wait_ge(s_y2, NT * p + i + 1)
                nc.scalar.activation(ysq[:, p, T * i:T * i + T], y2[:, p, T * i:T * i + T], ACT.Square)\
                    .then_inc(s_ysq, 1)

            def squeeze(p):
                act.wait_ge(s_hidp, p + 1)
                nc.scalar.activation(hidden[:, p:p + 1], ps_se[0:BP * HID, 0:1], ACT.Relu, scale=2.0 / N,
                                     bias=pl[0:BP * HID, L_SE1B:L_SE1B + 1]).then_inc(s_hid, 1)

            def excite(p):
                act.wait_ge(s_gatep, p + 1)
                nc.scalar.activation(gate_t[:, p:p + 1], ps_se[:, 1:2], ACT.Tanh, scale=0.5,
                                     bias=half_bias[:, 1:2]).then_inc(s_gatet, 1)

            group_norm(1)
            keys_copy(0)
            keys_copy(1)
            softmax(0, 0)
            values_copy(0)
            softmax(0, 1)
            values_copy(1)
            probT_copy(0, 0)
            probT_copy(0, 1)
            softmax(1, 0)
            softmax(1, 1)
            h_copy(0)
            probT_copy(1, 0)
            probT_copy(1, 1)
            layer_affine(0)
            layer_affine_delayed(0)
            dt_exp(0)
            conv_silu(0)
            c_copy(0)
            gate_tanh(0)
            h_copy(1)
            layer_affine(1)
            decays(0, 0)
            decays(0, 1)
            dt_exp(1)
            decays(0, 2)
            decays(0, 3)
            chunk_state(0)
            square(0, 0)
            conv_silu(1)
            square(0, 1)
            decays(1, 0)
            c_copy(1)
            gate_tanh(1)
            decays(1, 1)
            decays(1, 2)
            decays(1, 3)
            chunk_state(1)
            square(1, 0)
            squeeze(0)
            excite(0)
            square(1, 1)
            squeeze(1)
            excite(1)

        @block.vector
        def _(dve):
            done = [0]

            def link(ins):
                done[0] += 1
                ins.then_inc(s_vec, 1)
                dve.wait_ge(s_vec, done[0])

            for p in range(PAIRS):
                dve.wait_ge(s_x[p], 16)
                nc.vector.bn_stats(gst[:, p, :], xc[:, p, :]).then_inc(s_vec, 1)
                done[0] += 1
            for p in range(PAIRS):
                dve.wait_ge(s_vec, p + 1)
                nc.vector.bn_aggr(gmv[:, p, 0:2], gst[:, p, :]).then_inc(s_vec, 1)
                done[0] += 1
            dve.wait_ge(s_vec, done[0])
            nc.vector.tensor_tensor(gmv[:, :, 2], gmv[:, :, 0], gmv[:, :, 0], ALU.mult).then_inc(s_gsq, 1)
            dve.wait_ge(s_gg, 1)
            nc.vector.tensor_copy(gg[:, :, :].rearrange("p b m -> p (b m)"), ps_group[:, 0:3 * PAIRS])\
                .then_inc(s_gread, 1)
            dve.wait_ge(s_gread, 1)
            nc.vector.tensor_tensor(ggsq[:, :], gg[:, :, 0], gg[:, :, 0], ALU.mult).then_inc(s_vec, 1)
            done[0] += 1
            link(nc.vector.tensor_tensor(gms[:, :], gg[:, :, 1], gg[:, :, 2], ALU.add))
            nc.vector.scalar_tensor_tensor(gve[:, :], gms[:, :], EPS, ggsq[:, :], ALU.add, ALU.subtract)\
                .then_inc(s_gve, 1)
            for p in (1, 0):
                nc.vector.tensor_scalar(xm[:, p, :], xc[:, p, :], gg[:, p, 0:1], None, ALU.subtract)\
                    .then_inc(s_xm, 1)
            dve.wait_ge(s_early, 16)
            dve.wait_ge(s_gscale, 1)
            dve.wait_ge(s_xm, 2)
            nc.vector.tensor_scalar(xn[:, 0, :], xm[:, 0, :], gscale[:, 0:1], pe_[:, E_BETA:E_BETA + 1],
                                    ALU.mult, ALU.add).then_inc(s_xn0, 1)

            def tokens(p):
                dve.wait_ge(s_xTp, PAIRS)
                nc.vector.tensor_tensor(
                    xT[:, p, :, :], ps_xT[:, N * p:N * p + N].rearrange("p (k c) -> p k c", k=K),
                    pe_[:, E_BPROJ:E_BPROJ + C].unsqueeze(1).to_broadcast([128, K, C]), ALU.add)\
                    .then_inc(s_xT, 1)

            def keys_copy(p):
                dve.wait_ge(s_keysp, p + 1)
                if p == 0:
                    dve.wait_ge(s_pad, 1)
                nc.vector.tensor_scalar(keys[C:2 * C, p, 1, :], ps_keys[p][C:2 * C, 0:N], C ** -0.5, None,
                                        ALU.mult).then_inc(s_keys[1], 1)

            def row_max(p, b):
                dve.wait_ge(s_score, NT * (BP * p + b) + NT)
                nc.vector.tensor_reduce(neg_max[:, p, b, :], ps_score[b][:, :].rearrange("p (i m) -> p i m", i=NT),
                                        AX.X, ALU.max, negate=True).then_inc(s_max, 1)

            def residual(p, b):
                dve.wait_ge(s_y, BP * p + b + 1)
                yv = ps_y[b][:, 0:NT * (C + 1)].rearrange("p (i c) -> p i c", i=NT)
                link(nc.vector.reciprocal(rden[:, p, b, :], yv[:, :, C]))
                dve.wait_ge(s_xT, PAIRS)
                for i in range(NT):
                    k = BP * i + b
                    nc.vector.scalar_tensor_tensor(h[:, p, k, :], yv[:, i, 0:C], rden[:, p, b, i:i + 1],
                                                   xT[:, p, k, :], ALU.mult, ALU.add).then_inc(s_h, 1)

            def layer_stats(p, b):
                done_h, done_bn = NT * (BP * p + b), 2 * NT * (BP * p + b)
                for i in range(NT):
                    dve.wait_ge(s_h, done_h + i + 1)
                    nc.vector.bn_stats(lst[:, p, BP * i + b, :], h[:, p, BP * i + b, :]).then_inc(s_bn, 1)
                for i in range(NT):
                    dve.wait_ge(s_bn, done_bn + i + 1)
                    nc.vector.bn_aggr(lmv[:, p, BP * i + b, :], lst[:, p, BP * i + b, :]).then_inc(s_bn, 1)
                dve.wait_ge(s_bn, done_bn + 2 * NT)
                nc.vector.tensor_scalar(lve[:, p, b, :], lmv[:, p, b:K:BP, 1], EPS, None, ALU.add)\
                    .then_inc(s_lve, 1)

            def layer_scale(p, b):
                dve.wait_ge(s_lrs, BP * p + b + 1)
                for i in range(NT):
                    k = BP * i + b
                    nc.vector.tensor_scalar(u[:, p, k, :, :],
                                            h[:, p, k, :].unsqueeze(1).to_broadcast([128, 2, C]), lmv[:, p, k, 0:1],
                                            lrs[:, p, b, i:i + 1], ALU.subtract, ALU.mult).then_inc(s_u, 1)

            def layer_affine(p):
                if p == 0:
                    dve.wait_ge(s_zero, 8)
                dve.wait_ge(s_uTp, p + 1)
                nc.vector.tensor_scalar(uc[C:2 * C, p, :, TAPS - 2:TAPS - 2 + N],
                                        ps_uT[C:2 * C, :].rearrange("p (b n) -> p b n", b=BP),
                                        pl[C:2 * C, L_NG:L_NG + 1], pl[C:2 * C, L_NB:L_NB + 1],
                                        ALU.mult, ALU.add).then_inc(s_uchi, 1)

            def taps():
                dve.wait_ge(s_late, 16)
                dve.wait_ge(s_ident, 1)
                nc.vector.tensor_tensor(
                    conv_in[:, :, :], pl[:, L_INW:L_INW + C].unsqueeze(1).to_broadcast([128, TAPS, C]),
                    pl[:, L_CONVW:L_CONVW + TAPS].unsqueeze(2).to_broadcast([128, TAPS, C]), ALU.mult)\
                    .then_inc(s_convin, 1)
                nc.vector.tensor_scalar(diag_d[:, :], ident[:, 0:C], pl[:, L_D:L_D + 1], None, ALU.mult)\
                    .then_inc(s_diag, 1)

            def weights():
                dve.wait_ge(s_wconvp, 1)
                nc.vector.tensor_copy(conv_w[:, :, :].rearrange("p k c -> p (k c)"), ps_setup[:, 0:256])\
                    .then_inc(s_wconv, 1)
                dve.wait_ge(s_zero, 9)
                dve.wait_ge(s_half, 2)
                for b in range(BP):
                    rows = slice(C * b, C * b + C)
                    nc.vector.tensor_scalar(outw[rows, b, 0:C], pl[rows, L_OUTWT:L_OUTWT + C], rms_gain[rows, :],
                                            None, ALU.mult).then_inc(s_outw, 1)
                    nc.vector.tensor_scalar(outw[rows, b, C:OC], ps_setup[rows, 256:256 + HID], rms_gain[rows, :],
                                            None, ALU.mult).then_inc(s_outw, 1)

            def dt_argument(p):
                dve.wait_ge(s_dtp, p + 1)
                nc.vector.tensor_tensor(dx[:, p, :, :], ps_dt[:, 0:K * NH].rearrange("p (k h) -> p k h", k=K),
                                        pl[:, L_DTB:L_DTB + NH].unsqueeze(1).to_broadcast([128, K, NH]),
                                        ALU.add).then_inc(s_dx, 1)

            def dt_magnitude(p):
                dve.wait_ge(s_dx, p + 1)
                dxf = dx[:, p, :, :].rearrange("p k h -> p (k h)")
                nc.vector.scalar_tensor_tensor(dn[:, p, :], dxf, -1.0, dxf, ALU.mult, ALU.min)\
                    .then_inc(s_dn, 1)

            def softplus(p, step):
                e, d, r, z, w = de[:, p, :], dd[:, p, :], dr[:, p, :], dz[:, p, :], dw[:, p, :]
                q = [dq[:, p, 0, :], dq[:, p, 1, :]]
                if step == 0:
                    dve.wait_ge(s_de, p + 1)
                else:
                    dve.wait_ge(s_softplus, SOFTPLUS * p + step)
                if step == 0:
                    ins = nc.vector.tensor_scalar(d, e, 2.0, None, ALU.add)
                elif step == 1:
                    ins = nc.vector.reciprocal(r, d)
                elif step == 2:
                    ins = nc.vector.tensor_tensor(z, e, r, ALU.mult)
                elif step == 3:
                    ins = nc.vector.tensor_tensor(w, z, z, ALU.mult)
                elif step == 4:
                    ins = nc.vector.tensor_scalar(q[0], w, ART[4], None, ALU.mult)
                elif step < 8:
                    ins = nc.vector.scalar_tensor_tensor(q[step % 2 == 1], q[step % 2 == 0], ART[8 - step], w,
                                                         ALU.add, ALU.mult)
                elif step == 8:
                    ins = nc.vector.scalar_tensor_tensor(q[0], q[1], ART[0], z, ALU.add, ALU.mult)
                elif step == 9:
                    ins = nc.vector.scalar_tensor_tensor(dt[:, p, :, :].rearrange("p k h -> p (k h)"),
                                                         dx[:, p, :, :].rearrange("p k h -> p (k h)"), 0.0, q[0],
                                                         ALU.max, ALU.add)
                else:
                    if p == 0:
                        dve.wait_ge(s_nega, 1)
                    ins = nc.vector.tensor_tensor(a[:, p, :, :], dt[:, p, :, :],
                                                  neg_a[:, :].unsqueeze(1).to_broadcast([128, K, NH]), ALU.mult)
                ins.then_inc(s_softplus, 1)

            def conv_silu(p):
                dve.wait_ge(s_half_t, p + 1)
                dve.wait_ge(s_half_v, p + 1)
                nc.vector.scalar_tensor_tensor(s[:, p, :, :], half_t[:, p, :, :], 1.0, half_v[:, p, :, :],
                                               ALU.add, ALU.mult).then_inc(s_s, 1)

            def gate_silu(p):
                dve.wait_ge(s_zt, p + 1)
                nc.vector.scalar_tensor_tensor(zg[:, p, :], zt[:, p, :], 1.0, ps_z[:, N:2 * N],
                                               ALU.add, ALU.mult).then_inc(s_zg, 1)

            def own_columns(p):
                flat = dtx[:, p, :, :, :].rearrange("p k h c -> p k (h c)")
                pad = flat[:, :, 0:NH * (C + HD) - C]
                return bass.AP(pad.tensor, pad.offset, [list(pad.ap[0]), list(pad.ap[1]), [C + HD, NH], [1, HD]])

            def token_inputs(p):
                dve.wait_ge(s_sT, p + 1)
                dve.wait_ge(s_softplus, SOFTPLUS * p + 10)
                if p == 0:
                    dve.wait_ge(s_pad, 5)
                tv = ps_sT[:, :].rearrange("p (k c) -> p k c", k=K)
                nc.vector.tensor_tensor(
                    own_columns(p),
                    tv[:, :, 0:C].rearrange("p k (h d) -> p k h d", h=NH),
                    dt[:, p, :, :].unsqueeze(3).to_broadcast([128, K, NH, HD]), ALU.mult).then_inc(s_dtx, 1)
                nc.vector.tensor_copy(bT[:, p, :, :], tv[:, 0:BP, C:C + DS]).then_inc(s_bT, 1)

            def mask_products(p):
                dve.wait_ge(s_G, p + 1)
                if p == 0:
                    dve.wait_ge(s_masks, 2)
                nc.vector.tensor_tensor(gm[:, p, :, :], ps_G[:, :].rearrange("p (k t) -> p k t", k=K),
                                        upto[:, :].unsqueeze(1).to_broadcast([128, K, T]), ALU.mult)\
                    .then_inc(s_gm, 1)
                dve.wait_ge(s_gm, p + 1)

            def weigh(p, k):
                dve.wait_ge(s_decay, K * p + k + 1)
                nc.vector.tensor_tensor(att[:, p, k, :, :], decay[:, p, k, :, :],
                                        gm[:, p, k, :].unsqueeze(1).to_broadcast([128, NH, T]), ALU.mult)\
                    .then_inc(s_att, 1)

            def state_inputs(p):
                dve.wait_ge(s_decay, K * p + BP)
                dve.wait_ge(s_dtx, p + 1)
                nc.vector.tensor_tensor(
                    wdtx[:, p, :, :].rearrange("p b (h d) -> p b h d", h=NH), own_columns(p)[:, 0:BP, :, :],
                    decay[:, p, 0:BP, :, T - 1:T].to_broadcast([128, BP, NH, HD]), ALU.mult)\
                    .then_inc(s_wdtx, 1)

            def carried(p):
                dve.wait_ge(s_inter, p + 1)
                dve.wait_ge(s_carry, p + 1)
                nc.vector.tensor_tensor(yc[:, p, :], ps_mid[:, 128:128 + T], carry[:, p, :], ALU.mult)\
                    .then_inc(s_yc, 1)

            def gated(p, i):
                dve.wait_ge(s_ys, NT * p + i + 1)
                dve.wait_ge(s_zg, p + 1)
                at = slice(T * i, T * i + T)
                nc.vector.tensor_tensor(y2[:, p, at], ps_ys[i][:, 0:T], zg[:, p, at], ALU.mult).then_inc(s_y2, 1)

            def sum_of_squares(p, i):
                dve.wait_ge(s_o, NT * p + i + 1)
                nc.vector.tensor_scalar(yve[:, p, BP * i:BP * i + BP], ps_o[i][:, BP * OC:BP * OC + BP],
                                        4 * EPS * C, None, ALU.add).then_inc(s_yve, 1)

            def rms_scale(p, i):
                dve.wait_ge(s_yrs, NT * p + i + 1)
                rs = yrs[:, p, BP * i:BP * i + BP].unsqueeze(2)
                ov = ps_o[i][:, 0:BP * OC].rearrange("p (b c) -> p b c", b=BP)
                nc.vector.tensor_tensor(q3[:, p, i, :].rearrange("p (b c) -> p b c", b=BP), ov[:, :, C:OC],
                                        rs.to_broadcast([128, BP, HID]), ALU.mult).then_inc(s_q3, 1)
                nc.vector.tensor_tensor(o3[:, p, i, :].rearrange("p (b c) -> p b c", b=BP), ov[:, :, 0:C],
                                        rs.to_broadcast([128, BP, C]), ALU.mult).then_inc(s_o3, 1)

            def finish(p):
                dve.wait_ge(s_outp, NT * (p + 1))
                dve.wait_ge(s_hT, p + 1)
                link(nc.vector.tensor_tensor(base[:, p, :], ps_out[:, 0:N], hT[:, p, :], ALU.add))
                dve.wait_ge(s_gatet, p + 1)
                nc.vector.scalar_tensor_tensor(res[:, p, :], ps_out[:, 0:N], gate_t[:, p:p + 1], base[:, p, :],
                                               ALU.mult, ALU.add).then_inc(s_res, 1)

            keys_copy(0)
            taps()
            keys_copy(1)
            tokens(0)
            tokens(1)
            row_max(0, 0)
            row_max(0, 1)
            row_max(1, 0)
            weights()
            row_max(1, 1)
            residual(0, 0)
            layer_stats(0, 0)
            residual(0, 1)
            layer_stats(0, 1)
            layer_scale(0, 0)
            layer_scale(0, 1)
            residual(1, 0)
            layer_stats(1, 0)
            residual(1, 1)
            layer_stats(1, 1)
            dt_argument(0)
            dt_magnitude(0)
            softplus(0, 0)
            softplus(0, 1)
            softplus(0, 2)
            softplus(0, 3)
            softplus(0, 4)
            softplus(0, 5)
            softplus(0, 6)
            softplus(0, 7)
            softplus(0, 8)
            softplus(0, 9)
            softplus(0, 10)
            layer_scale(1, 0)
            conv_silu(0)
            layer_scale(1, 1)
            token_inputs(0)
            gate_silu(0)
            layer_affine(1)
            mask_products(0)
            dt_argument(1)
            dt_magnitude(1)
            state_inputs(0)
            weigh(0, 0)
            weigh(0, 1)
            weigh(0, 2)
            softplus(1, 0)
            softplus(1, 1)
            softplus(1, 2)
            softplus(1, 3)
            softplus(1, 4)
            weigh(0, 3)
            softplus(1, 5)
            softplus(1, 6)
            softplus(1, 7)
            gated(0, 0)
            softplus(1, 8)
            softplus(1, 9)
            softplus(1, 10)
            carried(0)
            gated(0, 1)
            sum_of_squares(0, 0)
            conv_silu(1)
            gate_silu(1)
            rms_scale(0, 0)
            sum_of_squares(0, 1)
            token_inputs(1)
            mask_products(1)
            rms_scale(0, 1)
            state_inputs(1)
            weigh(1, 0)
            weigh(1, 1)
            weigh(1, 2)
            weigh(1, 3)
            gated(1, 0)
            carried(1)
            sum_of_squares(1, 0)
            rms_scale(1, 0)
            finish(0)
            gated(1, 1)
            sum_of_squares(1, 1)
            rms_scale(1, 1)
            finish(1)

        @block.tensor
        def _(pe):
            mm = nc.tensor.matmul

            def keep_busy(where, *stage):
                columns = WARM.get(stage, 0)
                while columns > 0:
                    mm(where[:, 0:min(columns, 512)], busy[:, 0:128], busy[:, 0:min(columns, 512)],
                       start=True, stop=True)
                    columns -= 512

            pe.wait_ge(s_busy, 1)
            keep_busy(ps_setup, "start", 0)
            pe.wait_ge(s_group, 2)
            pe.wait_ge(s_gsq, 1)
            mm(ps_group[:, 0:3 * PAIRS], group_mean[:, :], gmv[:, :, :].rearrange("p b m -> p (b m)"),
               start=True, stop=True).then_inc(s_gg, 1)
            pe.wait_ge(s_early, 16)
            mm(ps_setup[:, 0:C], pe_[0:C, E_WK:E_WK + 2 * C], pe_[0:C, E_WQ:E_WQ + C], start=True, stop=True)
            mm(ps_setup[:, C:2 * C], pe_[0:C, E_WV:E_WV + 2 * C], pe_[0:C, E_WPT:E_WPT + C],
               start=True, stop=True).then_inc(s_mixp, 1)
            pe.wait_ge(s_ident, 1)
            for p in range(PAIRS):
                pe.wait_ge(s_x[p], 16)
                for i in range(NT):
                    last = nc.tensor.transpose(ps_xT[:, (NT * p + i) * T:(NT * p + i + 1) * T],
                                               xc[:, p, T * i:T * i + T], ident[:, :])
                last.then_inc(s_xTp, 1)
            keep_busy(ps_keys[0], "group", 0)

            def project_keys(p):
                if p == 0:
                    pe.wait_ge(s_mix, BP)
                pe.wait_ge([s_xn0, s_xn1][p], 1)
                mm(ps_keys[p][:, 0:N], mix[:, 0, :], xn[:, p, :], start=True, stop=True).then_inc(s_keysp, 1)

            def project_values(p):
                if p == 0:
                    pe.wait_ge(s_gread, 1)
                pe.wait_ge([s_xn0, s_xn1][p], 1)
                for i in range(NT):
                    last = mm(ps_vals[p][:, T * i:T * i + T], xn[:, p, T * i:T * i + T], mix[:, 1, :],
                              start=True, stop=True)
                last.then_inc(s_valsp, 1)

            def scores(p, b):
                if p > 0:
                    pe.wait_ge(s_prob, NT * (b + 1))
                pe.wait_ge(s_keys[b], p + 1)
                for i in range(NT):
                    mm(ps_score[b][:, N * i:N * i + N], xn[:, p, T * i:T * i + T], keys[:, p, b, :],
                       start=True, stop=True).then_inc(s_score, 1)

            def transpose_prob(p, b):
                if p > 0:
                    pe.wait_ge(s_probT, BP * (p - 1) + b + 1)
                elif b == 1:
                    pe.wait_ge(s_vals, PAIRS)
                else:
                    for copied in s_keys:
                        pe.wait_ge(copied, PAIRS)
                keep_busy(ps_probT[b], "transpose_prob", p, b)
                for i in range(NT):
                    pe.wait_ge(s_prob, NT * (BP * p + b) + i + 1)
                    for j in range(NT):
                        last = nc.tensor.transpose(ps_probT[b][:, N * j + T * i:N * j + T * i + T],
                                                   prob[:, p, b, i, T * j:T * j + T], ident[:, :])
                last.then_inc(s_probTp, 1)

            def attend(p, b):
                if b == 0:
                    pe.wait_ge(s_vals, PAIRS)
                    if p == 0:
                        pe.wait_ge(s_zero, 9)
                    else:
                        pe.wait_ge(s_hT, p)
                    keep_busy(ps_y[0], "attend", p)
                elif p == 0:
                    pe.wait_ge(s_wconv, 1)
                    pe.wait_ge(s_outw, 2 * BP)
                else:
                    pe.wait_ge(s_h, K * p)
                pe.wait_ge(s_probT, BP * p + b + 1)
                for i in range(NT):
                    for j in range(NT):
                        last = mm(ps_y[b][:, (C + 1) * i:(C + 1) * (i + 1)], probT[:, p, b, j, T * i:T * i + T],
                                  vals[:, p, BP * j + b, :], start=(j == 0), stop=(j == NT - 1))
                last.then_inc(s_y, 1)

            def transpose_h(p):
                pe.wait_ge(s_h, K * (p + 1))
                for i in range(NT):
                    last = nc.tensor.transpose(ps_hT[:, T * i:T * i + T],
                                               h[:, p, BP * i:BP * i + BP, :].rearrange("p b c -> p (b c)"),
                                               ident[:, :])
                last.then_inc(s_hTp, 1)

            def weights():
                pe.wait_ge(s_convin, 1)
                pe.wait_ge(s_mix, BP)
                for j in range(2):
                    nc.tensor.transpose(ps_setup[:, T * j:T * j + T],
                                        conv_in[:, 2 * j:2 * j + 2, :].rearrange("p k c -> p (k c)"),
                                        ident[:, :])
                mm(ps_setup[:, 256:256 + HID], pl[0:C, L_OUTW:L_OUTW + 2 * C], pl[0:C, L_SE1T:L_SE1T + HID],
                   start=True, stop=True).then_inc(s_wconvp, 1)

            def transpose_u(p):
                if p == 0:
                    pe.wait_ge(s_xT, PAIRS)
                else:
                    pe.wait_ge(s_bT, p)
                keep_busy(ps_uT, "transpose_u", p)
                for n in range(K):
                    b, i = divmod(n, NT)
                    pe.wait_ge(s_u, K * p + n + 1)
                    last = nc.tensor.transpose(ps_uT[:, N * b + T * i:N * b + T * i + T],
                                               u[:, p, BP * i + b, :, :].rearrange("p j c -> p (j c)"),
                                               ident[:, :])
                last.then_inc(s_uTp, 1)

            def project_dt(p):
                if p == 0:
                    for copied in s_keys:
                        pe.wait_ge(copied, 1)
                else:
                    pe.wait_ge(s_zg, p)
                keep_busy(ps_dt, "project_dt", p)
                pe.wait_ge(s_uclo, p + 1)
                for k in range(K):
                    i, b = divmod(k, BP)
                    at = TAPS - 1 + T * i
                    last = mm(ps_dt[:, NH * k:NH * k + NH], uc[0:C, p, b, at:at + T],
                              pl[0:C, L_WDT:L_WDT + NH], start=True, stop=True)
                last.then_inc(s_dtp, 1)

            def project_z(p):
                pe.wait_ge(s_dx, p + 1)
                pe.wait_ge(s_uchi, p + 1)
                for b in range(BP):
                    last = mm(ps_z[C * b:C * b + C, N:2 * N], pl[:, L_WZ:L_WZ + C],
                              uc[:, p, b, TAPS - 1:TAPS - 1 + N], start=True, stop=True)
                last.then_inc(s_zp, 1)

            def convolve(p):
                pe.wait_ge(s_uclo, p + 1)
                pe.wait_ge(s_uchi, p + 1)
                if p == 0:
                    pe.wait_ge(s_wconv, 1)
                    pe.wait_ge(s_h, K * PAIRS)
                else:
                    pe.wait_ge(s_gm, p)
                for j in range(2):
                    last = mm(ps_conv[:, :], conv_w[:, j, :], uc[:, p, :, 2 * j:2 * j + N],
                              start=(j == 0), stop=(j == 1))
                last.then_inc(s_conv, 1)

            def transpose_s(p):
                pe.wait_ge(s_uclo, p + 1)
                pe.wait_ge(s_uchi, p + 1)
                if p > 0:
                    pe.wait_ge(s_yc, p)
                keep_busy(ps_sT, "transpose_s", p)
                pe.wait_ge(s_s, p + 1)
                for k in range(K):
                    i, b = divmod(k, BP)
                    last = nc.tensor.transpose(ps_sT[:, T * k:T * k + T], s[:, p, b, T * i:T * i + T], ident[:, :])
                last.then_inc(s_sT, 1)

            def products(p):
                pe.wait_ge(s_cs, p + 1)
                for k in range(K):
                    i, b = divmod(k, BP)
                    last = mm(ps_G[:, T * k:T * k + T], s[:, p, b, T * i:T * i + T],
                              cs[:, p, b, T * i:T * i + T], start=True, stop=True)
                last.then_inc(s_G, 1)

            def segment_sums(p, k):
                if p == 0 and k == 0:
                    pe.wait_ge(s_masks, 1)
                    pe.wait_ge(s_prob, NT * B)
                    pe.wait_ge(s_probT, B)
                before = K * p + k - len(ps_S)
                if before >= 0:
                    pe.wait_ge(s_decay, before + 1)
                keep_busy(ps_S[(K * p + k) % len(ps_S)], "segment_sums", p, k)
                pe.wait_ge(s_am, K * p + k + 1)
                mm(ps_S[(K * p + k) % len(ps_S)][:, :], after[:, :], am[:, p, k, :, :].rearrange("p h t -> p (h t)"),
                   start=True, stop=True).then_inc(s_S, 1)

            def chunk_state(p):
                pe.wait_ge(s_bT, p + 1)
                keep_busy(ps_mid, "chunk_state", p)
                pe.wait_ge(s_wdtx, p + 1)
                for b in range(BP):
                    mm(ps_mid[C:C + DS, C * b:C * b + C], bT[:, p, b, :], wdtx[:, p, b, :],
                       start=True, stop=True)
                if p == 0:
                    pe.wait_ge(s_masks, 2)
                pe.wait_ge(s_awide, p + 1)
                mm(ps_mid[:, 256:256 + T], a_wide[:, p, :, :, :].rearrange("p b h d -> p (b h d)"), upto[:, :],
                   start=True, stop=True).then_inc(s_statep, 1)

            def carried(p):
                if p > 0:
                    pe.wait_ge(s_q3, NT * p)
                    pe.wait_ge(s_o3, NT * p)
                keep_busy(ps_ys[1], "carried", p)
                pe.wait_ge(s_state, p + 1)
                pe.wait_ge(s_carry, p + 1)
                for b in range(BP):
                    last = mm(ps_mid[C * b:C * b + C, 128:128 + T], state[:, p, b, :], cs[:, p, b, T:2 * T],
                              start=True, stop=True)
                last.then_inc(s_inter, 1)

            def chunk_output(p, k):
                i, b = divmod(k, BP)
                if k == 0:
                    if p == 0:
                        pe.wait_ge(s_diag, 1)
                        pe.wait_ge(s_hT, PAIRS)
                    pe.wait_ge(s_dtx, p + 1)
                if p > 0 and b == 0:
                    pe.wait_ge(s_q3, NT * (p - 1) + i + 1)
                    pe.wait_ge(s_o3, NT * (p - 1) + i + 1)
                if b == 0:
                    keep_busy(ps_ys[i], "chunk_output", p, i)
                    for other in range(BP):
                        mm(ps_ys[i][C * other:C * other + C, 0:T], diag_d[:, :], s[:, p, other, T * i:T * i + T],
                           start=True, stop=False)
                elif i > 0:
                    pe.wait_ge(s_yc, p + 1)
                    for other in range(BP):
                        mm(ps_ys[i][C * other:C * other + C, 0:T], ident[:, C * other:C * other + C], yc[:, p, :],
                           start=False, stop=(other == 0))
                rows = ps_ys[i][C * b:C * b + C, 0:T]
                pe.wait_ge(s_att, K * p + k + 1)
                for hd in range(NH):
                    last = mm(rows, dtx[:, p, k, hd, :], att[:, p, k, hd, :], start=False,
                              stop=(hd == NH - 1 and not (i > 0 and b == 0)))
                if b == BP - 1:
                    last.then_inc(s_ys, 1)

            def out_project(p, i):
                pe.wait_ge(s_y2, NT * p + i + 1)
                mm(ps_o[i][:, 0:BP * OC], y2[:, p, T * i:T * i + T], outw[:, :, :].rearrange("p b c -> p (b c)"),
                   start=True, stop=True)
                pe.wait_ge(s_ysq, NT * p + i + 1)
                mm(ps_o[i][:, BP * OC:BP * OC + BP], ysq[:, p, T * i:T * i + T], pl[:, L_PICK:L_PICK + BP],
                   start=True, stop=True).then_inc(s_o, 1)

            def transpose_out(p, i):
                if i == 0:
                    pe.wait_ge(s_gm, min(p + 2, PAIRS))
                    if p > 0:
                        pe.wait_ge(s_res, p)
                pe.wait_ge(s_o3, NT * p + i + 1)
                nc.tensor.transpose(ps_out[:, T * i:T * i + T], o3[:, p, i, :], ident[:, :]).then_inc(s_outp, 1)

            def squeeze(p):
                if p == 0:
                    pe.wait_ge(s_zg, PAIRS)
                else:
                    pe.wait_ge(s_gatet, p)
                pe.wait_ge(s_q3, NT * (p + 1))
                for i in range(NT):
                    last = mm(ps_se[0:BP * HID, 0:1], q3[:, p, i, :], ones[:, :], start=(i == 0),
                              stop=(i == NT - 1))
                last.then_inc(s_hidp, 1)

            def excite(p):
                pe.wait_ge(s_hid, p + 1)
                mm(ps_se[:, 1:2], pl[0:BP * HID, L_SE2T:L_SE2T + 128], hidden[:, p:p + 1],
                   start=True, stop=True).then_inc(s_gatep, 1)

            project_keys(0)
            project_keys(1)
            scores(0, 0)
            scores(0, 1)
            project_values(0)
            project_values(1)
            weights()
            scores(1, 0)
            transpose_prob(0, 0)
            transpose_prob(0, 1)
            scores(1, 1)
            attend(0, 0)
            attend(0, 1)
            transpose_prob(1, 0)
            transpose_prob(1, 1)
            transpose_h(0)
            attend(1, 0)
            attend(1, 1)
            transpose_u(0)
            project_dt(0)
            convolve(0)
            project_z(0)
            transpose_h(1)
            transpose_s(0)
            segment_sums(0, 0)
            transpose_u(1)
            products(0)
            segment_sums(0, 1)
            project_dt(1)
            segment_sums(0, 2)
            convolve(1)
            segment_sums(0, 3)
            project_z(1)
            chunk_state(0)
            chunk_output(0, 0)
            chunk_output(0, 1)
            carried(0)
            chunk_output(0, 2)
            out_project(0, 0)
            chunk_output(0, 3)
            segment_sums(1, 0)
            segment_sums(1, 1)
            transpose_s(1)
            products(1)
            out_project(0, 1)
            segment_sums(1, 2)
            segment_sums(1, 3)
            transpose_out(0, 0)
            chunk_state(1)
            chunk_output(1, 0)
            chunk_output(1, 1)
            carried(1)
            transpose_out(0, 1)
            out_project(1, 0)
            squeeze(0)
            chunk_output(1, 2)
            excite(0)
            chunk_output(1, 3)
            transpose_out(1, 0)
            out_project(1, 1)
            squeeze(1)
            transpose_out(1, 1)
            excite(1)


def kernel(**inputs):
    import numpy as np
    import concourse.bacc as bacc
    from concourse.bass_utils import run_bass_kernel_spmd

    f = {name: np.asarray(value) for name, value in inputs.items()}

    def column(v, rows=128):
        col = np.zeros((128, 1), np.float32)
        col[:rows, 0] = np.concatenate([v] * (rows // v.shape[0]))
        return col

    def row(v):
        return np.ascontiguousarray(np.broadcast_to(v[None, :], (128, v.shape[0])))

    def top(m):
        full = np.zeros((128, m.shape[1]), np.float32)
        full[:m.shape[0]] = m
        return full

    def twice(m):
        return np.concatenate([m, m], axis=1)

    def diagonal(m):
        r, c = m.shape
        full = np.zeros((128, BP * c), np.float32)
        for b in range(BP):
            full[r * b:r * b + r, c * b:c * b + c] = m
        return full

    w = f["L0_conv_w_qkv"]
    early = np.concatenate([
        column(f["L0_conv_gamma"]), column(f["L0_conv_beta"]),
        top(w[0:C]), top(twice(w[C:2 * C])), top(twice(w[2 * C:3 * C])), top(f["L0_conv_w_proj"].T),
        row(f["L0_conv_b_proj"])], axis=1)
    inw = f["L1_conv_in_w"]
    xbc = inw[C:C + 128]
    wz, wdt = inw[0:C], inw[C + 128:]
    late = np.concatenate([
        column(f["L1_conv_norm_g"]), column(f["L1_conv_norm_b"]), column(f["L1_conv_rms_w"]),
        column(np.repeat(f["L1_conv_Dp"], HD)), column(f["L1_conv_conv_b"]), column(f["L1_conv_se2_b"]),
        column(f["L1_conv_se1_b"], BP * HID), np.zeros((128, 1), np.float32),
        f["L1_conv_conv_w"], row(f["L1_conv_dt_bias"]), row(f["L1_conv_A_log"]),
        xbc, top(wz.T), top(wdt.T), top(twice(f["L1_conv_out_w"])), np.concatenate([f["L1_conv_out_w"].T] * BP),
        top(f["L1_conv_se1_w"].T), diagonal(f["L1_conv_se2_w"].T), diagonal(np.ones((C, 1), np.float32))], axis=1)

    fp32 = mybir.dt.float32
    nc = bacc.Bacc("TRN2", target_bir_lowering=False, num_devices=1)
    arrays = {"in_x": np.ascontiguousarray(f["x"]), "in_early": early, "in_late": late}
    args = [nc.dram_tensor(n, v.shape, fp32, kind="ExternalInput").ap() for n, v in arrays.items()]
    args.append(nc.dram_tensor("out_0", f["x"].shape, fp32, kind="ExternalOutput").ap())
    attention_mamba_kernel(nc, *args)
    r = run_bass_kernel_spmd(nc, [arrays], core_ids=[0])
    return r.results[0]["out_0"]
```
